# Optimizing a Trainium2 kernel written in Bass

```python
import numpy as np
import jax
import jax.numpy as jnp

def _softmax(x, axis=-1):
    return jax.nn.softmax(x, axis=axis)

def _gelu(x):
    return jax.nn.gelu(x, approximate=True)

def _silu(x):
    return jax.nn.silu(x)

def _sigmoid(x):
    return jax.nn.sigmoid(x)

def _layernorm(x, axis=-1, eps=1e-05):
    m = jnp.mean(x, axis=axis, keepdims=True)
    v = jnp.var(x, axis=axis, keepdims=True)
    return (x - m) / jnp.sqrt(v + eps)

def _scatter_add(tgt, idx, src, axis=0):
    return tgt.at[idx].add(src)

def _segment_sum(src, seg, n):
    return jax.ops.segment_sum(src, seg, n)
kernel_name = 'mk_gnn_resnorm_d2_gnn_r8_33d477'

def setup_inputs(seed: int=0):
    np.random.seed(seed)
    _w = jnp.asarray

    def _rec_inputs():
        import jax
        import jax.numpy as jnp
        _gk = jax.random.key(seed)
        x = -0.0005963 + 1.001 * jax.random.normal(jax.random.fold_in(_gk, 1), (384, 1024), jnp.float32)
        _s = jax.random.randint(jax.random.fold_in(_gk, 2), (3072,), 0, 384, jnp.int32)
        _d = jax.random.randint(jax.random.fold_in(_gk, 3), (3072,), 0, 384, jnp.int32)
        _loop = jnp.arange(384, dtype=jnp.int32)
        src = jnp.concatenate([_s, _d, _loop])
        dst = jnp.concatenate([_d, _s, _loop])
        _o = jnp.argsort(dst, stable=True)
        src = src[_o]
        dst = dst[_o]
        edge_type_5 = jax.random.randint(jax.random.fold_in(_gk, 12), (6528,), 0, 5, jnp.int32)
        edge_type_8 = jax.random.randint(jax.random.fold_in(_gk, 13), (6528,), 0, 8, jnp.int32)
        return (x, src, dst, edge_type_5, edge_type_8)
    x, src, dst, edge_type_5, edge_type_8 = _rec_inputs()

    def _L0_gnn_setup():
        import jax, jax.numpy as jnp
        import numpy as np
        N = 384
        E = 12288
        IN_F = 1024
        OUT_F = 1024
        H = 16
        D = OUT_F // H
        NUM_ETYPES = 4

        def _build_mask(edge_index, edge_type, edge_type_weights, dtype):
            src, dst = (edge_index[0], edge_index[1])
            w = jax.nn.softplus(edge_type_weights)
            mask = jnp.full((N, N), -jnp.inf, dtype=dtype)
            mask = mask.at[src, dst].set(w[edge_type - 1])
            diag = jnp.diagonal(mask)
            idx = jnp.arange(N)
            mask = mask.at[idx, idx].set(jnp.where(jnp.isneginf(diag), w[3], diag))
            return mask
        key = jax.random.key(seed)
        ks = jax.random.split(key, 20)
        p = lambda k, shape: jax.random.normal(k, shape, dtype=jnp.float32) * 0.02
        return {'x': jax.random.normal(ks[0], (N, IN_F), dtype=jnp.float32), 'edge_index': jax.random.randint(ks[1], (2, E), 0, N), 'edge_type': jax.random.randint(ks[2], (E,), 1, NUM_ETYPES + 1), 'edge_type_weights': jnp.ones((NUM_ETYPES,), jnp.float32) + 0.1 * jax.random.normal(ks[3], (NUM_ETYPES,), dtype=jnp.float32), 'wq': p(ks[4], (OUT_F, IN_F)), 'bq': p(ks[5], (OUT_F,)), 'wk': p(ks[6], (OUT_F, IN_F)), 'bk': p(ks[7], (OUT_F,)), 'wv': p(ks[8], (OUT_F, IN_F)), 'bv': p(ks[9], (OUT_F,)), 'wiq': p(ks[10], (OUT_F, OUT_F)), 'biq': p(ks[11], (OUT_F,)), 'wik': p(ks[12], (OUT_F, OUT_F)), 'bik': p(ks[13], (OUT_F,)), 'wiv': p(ks[14], (OUT_F, OUT_F)), 'biv': p(ks[15], (OUT_F,)), 'wo': p(ks[16], (OUT_F, OUT_F)), 'bo': p(ks[17], (OUT_F,))}
    _L0_gnn_all = _L0_gnn_setup()
    _L0_gnn_in = {k: v for k, v in _L0_gnn_all.items() if k in ('edge_type_weights', 'wq', 'bq', 'wk', 'bk', 'wv', 'bv', 'wiq', 'biq', 'wik', 'bik', 'wiv', 'biv', 'wo', 'bo')}
    del _L0_gnn_all

    def _L1_gnn_setup():
        import jax, jax.numpy as jnp
        import numpy as np
        N, D, R, E = (1250, 1024, 8, 10000)

        def _rgcn(x, edge_index, edge_type, weight, root, bias):
            src, dst = (edge_index[0], edge_index[1])
            msgs = x[src]
            out = x @ root + bias
            n = x.shape[0]
            for r in range(weight.shape[0]):
                mask = (edge_type == r).astype(x.dtype)
                sums = jax.ops.segment_sum(msgs * mask[:, None], dst, num_segments=n)
                cnt = jax.ops.segment_sum(mask, dst, num_segments=n)
                mean = sums / jnp.maximum(cnt, 1.0)[:, None]
                out = out + mean @ weight[r]
            return out
        key = jax.random.key(seed)
        ks = jax.random.split(key, 8)
        s = 1.0 / np.sqrt(D)
        x = jax.random.normal(ks[0], (N, D), dtype=jnp.float32)
        edge_index = jax.random.randint(ks[1], (2, E), 0, N, dtype=jnp.int64)
        edge_type = jax.random.randint(ks[2], (E,), 0, R, dtype=jnp.int64)
        weight = jax.random.normal(ks[3], (R, D, D), dtype=jnp.float32) * s
        root = jax.random.normal(ks[4], (D, D), dtype=jnp.float32) * s
        bias = jnp.zeros((D,), dtype=jnp.float32)
        w_gate = jax.random.normal(ks[5], (2 * D, D), dtype=jnp.float32) * (1.0 / np.sqrt(2 * D))
        b_gate = jnp.zeros((D,), dtype=jnp.float32)
        return {'x': x, 'edge_index': edge_index, 'edge_type': edge_type, 'weight': weight, 'root': root, 'bias': bias, 'w_gate': w_gate, 'b_gate': b_gate}
    _L1_gnn_all = _L1_gnn_setup()
    _L1_gnn_in = {k: v for k, v in _L1_gnn_all.items() if k in ('weight', 'root', 'bias', 'w_gate', 'b_gate')}
    del _L1_gnn_all
    return {'x': x, 'src': src, 'dst': dst, 'edge_type_5': edge_type_5, 'edge_type_8': edge_type_8, 'L0_gnn_edge_type_weights': _L0_gnn_in['edge_type_weights'], 'L0_gnn_wq': _L0_gnn_in['wq'], 'L0_gnn_bq': _L0_gnn_in['bq'], 'L0_gnn_wk': _L0_gnn_in['wk'], 'L0_gnn_bk': _L0_gnn_in['bk'], 'L0_gnn_wv': _L0_gnn_in['wv'], 'L0_gnn_bv': _L0_gnn_in['bv'], 'L0_gnn_wiq': _L0_gnn_in['wiq'], 'L0_gnn_biq': _L0_gnn_in['biq'], 'L0_gnn_wik': _L0_gnn_in['wik'], 'L0_gnn_bik': _L0_gnn_in['bik'], 'L0_gnn_wiv': _L0_gnn_in['wiv'], 'L0_gnn_biv': _L0_gnn_in['biv'], 'L0_gnn_wo': _L0_gnn_in['wo'], 'L0_gnn_bo': _L0_gnn_in['bo'], 'L1_gnn_weight': _L1_gnn_in['weight'], 'L1_gnn_root': _L1_gnn_in['root'], 'L1_gnn_bias': _L1_gnn_in['bias'], 'L1_gnn_w_gate': _L1_gnn_in['w_gate'], 'L1_gnn_b_gate': _L1_gnn_in['b_gate']}

def reference(x, src, dst, edge_type_5, edge_type_8, L0_gnn_edge_type_weights, L0_gnn_wq, L0_gnn_bq, L0_gnn_wk, L0_gnn_bk, L0_gnn_wv, L0_gnn_bv, L0_gnn_wiq, L0_gnn_biq, L0_gnn_wik, L0_gnn_bik, L0_gnn_wiv, L0_gnn_biv, L0_gnn_wo, L0_gnn_bo, L1_gnn_weight, L1_gnn_root, L1_gnn_bias, L1_gnn_w_gate, L1_gnn_b_gate):
    import jax
    import jax.numpy as jnp

    def _L0_gnn_ref(x, edge_index, edge_type, edge_type_weights, wq, bq, wk, bk, wv, bv, wiq, biq, wik, bik, wiv, biv, wo, bo):
        import jax, jax.numpy as jnp
        import numpy as np
        N = 384
        E = 12288
        IN_F = 1024
        OUT_F = 1024
        H = 16
        D = OUT_F // H
        NUM_ETYPES = 4

        def _build_mask(edge_index, edge_type, edge_type_weights, dtype):
            src, dst = (edge_index[0], edge_index[1])
            w = jax.nn.softplus(edge_type_weights)
            mask = jnp.full((N, N), -jnp.inf, dtype=dtype)
            mask = mask.at[src, dst].set(w[edge_type - 1])
            diag = jnp.diagonal(mask)
            idx = jnp.arange(N)
            mask = mask.at[idx, idx].set(jnp.where(jnp.isneginf(diag), w[3], diag))
            return mask
        q = x @ wq.T + bq
        k = x @ wk.T + bk
        v = x @ wv.T + bv
        q2 = (q @ wiq.T + biq).reshape(N, H, D).transpose(1, 0, 2)
        k2 = (k @ wik.T + bik).reshape(N, H, D).transpose(1, 0, 2)
        v2 = (v @ wiv.T + biv).reshape(N, H, D).transpose(1, 0, 2)
        mask = _build_mask(edge_index, edge_type, edge_type_weights, x.dtype)
        scale = 1.0 / np.sqrt(D).astype(np.float32)
        scores = jnp.einsum('hnd,hmd->hnm', q2, k2) * scale + mask[None]
        attn = jax.nn.softmax(scores, axis=-1)
        out = jnp.einsum('hnm,hmd->hnd', attn, v2)
        out = out.transpose(1, 0, 2).reshape(N, OUT_F)
        return out @ wo.T + bo

    def _L1_gnn_ref(x, edge_index, edge_type, weight, root, bias, w_gate, b_gate):
        import jax, jax.numpy as jnp
        import numpy as np
        N, D, R, E = (1250, 1024, 8, 10000)

        def _rgcn(x, edge_index, edge_type, weight, root, bias):
            src, dst = (edge_index[0], edge_index[1])
            msgs = x[src]
            out = x @ root + bias
            n = x.shape[0]
            for r in range(weight.shape[0]):
                mask = (edge_type == r).astype(x.dtype)
                sums = jax.ops.segment_sum(msgs * mask[:, None], dst, num_segments=n)
                cnt = jax.ops.segment_sum(mask, dst, num_segments=n)
                mean = sums / jnp.maximum(cnt, 1.0)[:, None]
                out = out + mean @ weight[r]
            return out
        u = _rgcn(x, edge_index, edge_type, weight, root, bias)
        z = jnp.concatenate([u, x], axis=1) @ w_gate + b_gate
        h = jnp.tanh(u) * z + x * (1.0 - z)
        return h
    edge_index = jnp.stack([src, dst])
    x = _layernorm(x + _L0_gnn_ref(x, edge_index, edge_type_5, L0_gnn_edge_type_weights, L0_gnn_wq, L0_gnn_bq, L0_gnn_wk, L0_gnn_bk, L0_gnn_wv, L0_gnn_bv, L0_gnn_wiq, L0_gnn_biq, L0_gnn_wik, L0_gnn_bik, L0_gnn_wiv, L0_gnn_biv, L0_gnn_wo, L0_gnn_bo), axis=-1)
    x = _layernorm(x + _L1_gnn_ref(x, edge_index, edge_type_8, L1_gnn_weight, L1_gnn_root, L1_gnn_bias, L1_gnn_w_gate, L1_gnn_b_gate), axis=-1)
    return x

_drawn_inputs = setup_inputs


def setup_inputs(seed=0):
    import zlib

    import numpy as np

    out = dict(_drawn_inputs(seed))
    spreads = {'L1_gnn_bias': (0.0, 0.1), 'L1_gnn_b_gate': (0.0, 0.1)}
    factors = {'L0_gnn_edge_type_weights': 7.133,
     'L0_gnn_wq': 4.044,
     'L0_gnn_bq': 8.0,
     'L0_gnn_wk': 4.031,
     'L0_gnn_bk': 8.0,
     'L0_gnn_bv': 4.884,
     'L0_gnn_wiq': 4.038,
     'L0_gnn_biq': 8.0,
     'L0_gnn_wik': 4.039,
     'L0_gnn_bik': 8.0,
     'L0_gnn_biv': 2.991}
    for name, (base, spread) in spreads.items():
        noise = np.random.default_rng([zlib.crc32(name.encode()), seed]).standard_normal(out[name].shape)
        drawn = base * np.exp(spread * noise) if base else spread * noise
        out[name] = jnp.asarray(drawn.astype(out[name].dtype))
    for name, factor in factors.items():
        out[name] = (out[name] * factor).astype(out[name].dtype)
    return out
```

```python
import concourse.bass as bass
from concourse import mybir
from contextlib import ExitStack

F32 = mybir.dt.float32
F32R = mybir.dt.float32r
BF16 = mybir.dt.bfloat16
F16 = mybir.dt.float16
I32 = mybir.dt.int32
ALU = mybir.AluOpType
ACT = mybir.ActivationFunctionType
AX = mybir.AxisListType

P = 128
N = 384
NT = N // P
D = 1024
KT = D // P
H = 16
DH = D // H
E = 6528
EC = E // P
R = 8
EPS = 1e-5
HALF = 512

UNIT = KT * P
RING = 4
U_F1 = 0
U_F2 = 3 * KT
U_WO = 6 * KT
U_ROOT = 7 * KT
U_REL = 8 * KT
U_GX = U_REL + R * KT
U_GU = U_GX + KT
UNITS = U_GU + KT

OH = 3
HALVES = ((0, 27), (27, EC))
FIELD = 4096
FIELD_BITS = 12
ABSENT = -1e30
SCORE_SCALE = 1.0 / (DH ** 0.5)


def build(nc, x_nat, x_t, edges, keys_src, keys_dst, type_w, bias_f, bo, bias, b_gate, weights, out):
    ctx = ExitStack()
    with ctx:
        base = nc.sbuf_base
        base = (base + 31) // 32 * 32
        place = [base]

        def region(size):
            at = place[0]
            place[0] += (size + 31) // 32 * 32
            return at

        def sb(name, cols, dt, at=None, parts=P):
            size = cols * (2 if dt in (BF16, F16) else 4)
            if at is None:
                at = region(size)
            return nc.alloc_sbuf_tensor_at(name, [parts, cols], dt, offset=at)

        raw = sb("raw", RING * UNIT, F32)
        w_hi = sb("w_hi", RING * UNIT, F32R)
        w_lo = sb("w_lo", RING * UNIT, F32R)

        ACTS = KT * N
        z1 = region(2 * 3 * ACTS * 4)
        z1b = z1 + 3 * ACTS * 4
        z2 = region(4 * ACTS * 4)
        onehots = region(2 * OH * N * 2)
        z3 = region(2 * ACTS * 4)

        t1_hi = sb("t1_hi", 3 * ACTS, F32R, z1)
        t1_lo = sb("t1_lo", 3 * ACTS, F32R, z1b)
        erow_at = z1b + (3 * ACTS - 16 * P) * 4
        erow_i = sb("erow_i", 4 * P, I32, erow_at, EC)
        erow_f = sb("erow_f", 4 * P, F32, erow_at + 4 * P * 4, EC)
        erow_s = sb("erow_s", 3 * P, I32, erow_at + 8 * P * 4, EC)
        v2t = sb("v2t", ACTS, F32, z1)
        logit = sb("logit", 2 * NT * N, F32, z1)
        prob = sb("prob", 2 * NT * N, F32, z1 + 2 * NT * N * 4)
        pt_hi = sb("pt_hi", 2 * NT * N, F32R, z1 + 4 * NT * N * 4)
        pt_lo = sb("pt_lo", 2 * NT * N, F32R, z1 + 6 * NT * N * 4)
        o_hi = sb("o_hi", ACTS, F32R, z1b)
        o_lo = sb("o_lo", ACTS, F32R, z1b + ACTS * 4)
        a_hi = sb("a_hi", R * NT * N, F32R, z1)
        a_lo = sb("a_lo", R * NT * N, F32R, z1b)
        u_nat = sb("u_nat", ACTS, F32, z1)
        gated = sb("gated", ACTS, F32, z1 + ACTS * 4)
        fixed = sb("fixed", ACTS, F32, z1 + 2 * ACTS * 4)
        ut_hi = sb("ut_hi", ACTS, F32R, z1b)
        ut_lo = sb("ut_lo", ACTS, F32R, z1b + ACTS * 4)
        result = sb("result", ACTS, F32, z1b + 2 * ACTS * 4)

        key_src = sb("key_src", E, I32, z2)
        key_row = sb("key_row", E, F32, z2)
        key_dst = sb("key_dst", E, I32, z2 + E * 4)
        t2_hi = sb("t2_hi", 2 * ACTS, F32R, z2)
        t2_lo = sb("t2_lo", 2 * ACTS, F32R, z2 + 2 * ACTS * 4)
        a_cnt = sb("a_cnt", R * NT * N, F32, z2)
        x1h_hi = sb("x1h_hi", ACTS, F32R, z2)
        x1h_lo = sb("x1h_lo", ACTS, F32R, z2 + ACTS * 4)
        mean_hi = sb("mean_hi", 2 * N, F32R, z2 + 2 * ACTS * 4)
        mean_lo = sb("mean_lo", 2 * N, F32R, z2 + 2 * ACTS * 4 + 2 * N * 4)
        x1 = sb("x1", ACTS, F32, z2 + 3 * ACTS * 4)

        xt_hi = sb("xt_hi", ACTS, F32R, z3)
        xt_lo = sb("xt_lo", ACTS, F32R, z3 + ACTS * 4)
        v2_hi = sb("v2_hi", ACTS, F32R, z3)
        v2_lo = sb("v2_lo", ACTS, F32R, z3 + ACTS * 4)
        both_i = sb("both_i", 2 * N, I32, z3)
        low_i = sb("low_i", N, I32, z3 + 2 * N * 4)
        high_i = sb("high_i", N, I32, z3 + 3 * N * 4)
        x1t_hi = sb("x1t_hi", ACTS, F32R, z3)
        x1t_lo = sb("x1t_lo", ACTS, F32R, z3 + ACTS * 4)
        rcount = sb("rcount", 2 * N, F32, onehots)

        src_oh = sb("src_oh", OH * N, BF16, onehots)
        dst_oh = sb("dst_oh", OH * N, BF16, onehots + OH * N * 2)

        mask_at = region(NT * N * 4)
        mask = sb("mask", NT * N, F32, mask_at)
        row_bias = sb("row_bias", D, F32, mask_at)
        m_code = sb("m_code", NT * N, I32, z1)
        m_kind = sb("m_kind", NT * N, I32, z1 + NT * N * 4)
        m_part = sb("m_part", NT * N, F32, z1 + 2 * NT * N * 4)

        xt_raw = sb("xt_raw", ACTS, F32, z1)

        iota_i = sb("iota_i", N, I32, mask_at)
        iota16 = sb("iota16", N, F16)
        ident = sb("ident", P, F32)
        ones = sb("ones", P, F32)
        later = sb("later", P, F32)
        cols = sb("cols", 4 * EC, F32)
        C_SRC, C_DST, C_CODE, C_REL = (i * EC for i in range(4))
        key_col = sb("key_col", EC, F32)
        dup = sb("dup", EC, F32)
        w_code = sb("w_code", EC, F32)
        w_rel = sb("w_rel", 4 * EC, F32)
        dup_junk = sb("dup_junk", P, F32)
        bias_col = sb("bias_col", 6 * KT, F32)
        tw = sb("tw", 4, F32)
        tw2 = sb("tw2", 4, F32)
        tw3 = sb("tw3", 4, F32)
        sm = sb("sm", 2 * 4 * NT, F32)
        stats = sb("stats", NT * 12, F32)
        mv = sb("mv", NT * 2, F32)
        rstd = sb("rstd", NT, F32)
        nhalf = sb("nhalf", NT, F32)
        vare = sb("vare", NT, F32)
        assert place[0] <= nc.sbuf_usable_end, (place[0], nc.sbuf_usable_end)

        bank = [ctx.enter_context(nc.psum_tensor(f"bank{i}", [P, HALF], F32)) for i in range(8)]

        def sem(name):
            return ctx.enter_context(nc.semaphore(name))

        raw_loaded = [sem(f"raw_loaded{j}") for j in range(RING)]
        hi_split = sem("hi_split")
        lo_split = sem("lo_split")
        unit_done = sem("unit_done")
        x_loaded = sem("x_loaded")
        small_loaded = sem("small_loaded")
        keys_loaded = sem("keys_loaded")
        const_made = sem("const_made")
        x_hi = sem("x_hi")
        x_ready = sem("x_ready")
        f_hi = sem("f_hi")
        f_lo = sem("f_lo")
        v_ev = sem("v_ev")
        rows_cast = sem("rows_cast")
        cols_turned = sem("cols_turned")
        dve = sem("dve")
        oh_ready = sem("oh_ready")
        oh_used = sem("oh_used")
        hist_cast = sem("hist_cast")
        hist_decoded = sem("hist_decoded")
        mask_made = sem("mask_made")
        tw_act = sem("tw_act")
        tw_dve = sem("tw_dve")
        v_turned = sem("v_turned")
        v_hi = sem("v_hi")
        v_ready = sem("v_ready")
        score_done = sem("score_done")
        logit_made = sem("logit_made")
        negmax = sem("negmax")
        exp_done = sem("exp_done")
        rsum = sem("rsum")
        prob_ready = sem("prob_ready")
        p_turned = sem("p_turned")
        pt_hi_made = sem("pt_hi_made")
        pt_ready = sem("pt_ready")
        pv_done = sem("pv_done")
        o_hi_made = sem("o_hi_made")
        o_ready = sem("o_ready")
        xres_loaded = sem("xres_loaded")
        bo_loaded = sem("bo_loaded")
        rb_loaded = sem("rb_loaded")
        bg_loaded = sem("bg_loaded")
        xb_made = sem("xb_made")
        res_made = sem("res_made")
        var_made = sem("var_made")
        rstd_made = sem("rstd_made")
        x1_made = sem("x1_made")
        x1_turned = sem("x1_turned")
        x1t_hi_made = sem("x1t_hi_made")
        x1t_ready = sem("x1t_ready")
        cnt_made = sem("cnt_made")
        cnt_summed = sem("cnt_summed")
        a_norm = sem("a_norm")
        a_hi_made = sem("a_hi_made")
        a_ready = sem("a_ready")
        x1h_hi_made = sem("x1h_hi_made")
        x1h_ready = sem("x1h_ready")
        agg_done = sem("agg_done")
        mean_hi_made = sem("mean_hi_made")
        mean_ready = sem("mean_ready")
        u_summed = sem("u_summed")
        u_made = sem("u_made")
        u_turned = sem("u_turned")
        ut_hi_made = sem("ut_hi_made")
        ut_ready = sem("ut_ready")
        tanh_made = sem("tanh_made")
        z_summed = sem("z_summed")
        out_made = sem("out_made")
        stored = sem("stored")

        CODE0 = 4

        def used_after(n):
            half, p = divmod(n, 4)
            return EC + 4 * sum(b - a for a, b in HALVES[:half]) + (p + 1) * (HALVES[half][1] - HALVES[half][0])

        block = ctx.enter_context(nc.Block())

        @block.sync
        def _(sp):
            sp.dma_start(xt_raw[:, :], x_t).then_inc(x_loaded, 16)
            for j in range(RING):
                sp.dma_start(raw[:, j * UNIT:(j + 1) * UNIT], weights[j]).then_inc(raw_loaded[j], 16)
            sp.dma_start(bias_col[:, :], bias_f).then_inc(small_loaded, 16)
            sp.dma_start(erow_i[:, :], edges).then_inc(small_loaded, 16)
            sp.dma_start(tw[:, :], type_w.partition_broadcast(P)).then_inc(small_loaded, 16)
            sp.dma_start(key_src[:, :], keys_src.partition_broadcast(P)).then_inc(keys_loaded, 16)
            sp.dma_start(key_dst[:, :], keys_dst.partition_broadcast(P)).then_inc(keys_loaded, 16)

            def load(u, j):
                sp.wait_ge(lo_split, u - RING + 1)
                sp.dma_start(raw[:, j * UNIT:(j + 1) * UNIT],
                             weights[bass.ds(u, 1)].rearrange("a p n -> (a p) n")).then_inc(raw_loaded[j], 16)

            with sp.Fori(1, U_WO // RING + 1) as i:
                for j in range(RING):
                    load(i * RING + j, j)
            sp.wait_ge(score_done, H * NT)
            sp.dma_start(x1[:, :], x_nat).then_inc(xres_loaded, 16)
            sp.wait_ge(logit_made, H * NT)
            sp.dma_start(row_bias[:, :], bo.partition_broadcast(P)).then_inc(bo_loaded, 16)
            with sp.Fori(U_WO // RING + 1, U_REL // RING) as i:
                for j in range(RING):
                    load(i * RING + j, j)
            sp.wait_ge(xb_made, 1)
            sp.dma_start(row_bias[:, :], bias.partition_broadcast(P)).then_inc(rb_loaded, 16)
            with sp.Fori(U_REL // RING, UNITS // RING) as i:
                for j in range(RING):
                    load(i * RING + j, j)
            sp.wait_ge(u_made, 2 * NT)
            sp.dma_start(row_bias[:, :], b_gate.partition_broadcast(P)).then_inc(bg_loaded, 16)
            for t in range(NT):
                sp.wait_ge(out_made, t + 1)
                sp.dma_start(out[t], result[:, t * D:(t + 1) * D]).then_inc(stored, 16)
            sp.wait_ge(stored, 16 * NT)

        @block.gpsimd
        def _(pool):
            g = nc.gpsimd
            g.memset(ident[:, :], 0.0).then_inc(const_made, 1)
            g.memset(ones[:, :], 1.0).then_inc(const_made, 1)
            g.memset(nhalf[:, :], -0.5).then_inc(const_made, 1)
            g.iota(iota_i[:, :], pattern=[[1, N]], base=0, channel_multiplier=0).then_inc(const_made, 1)
            g.iota(erow_s[:, 0:P], pattern=[[0, P]], base=CODE0, channel_multiplier=4).then_inc(const_made, 1)
            pool.wait_ge(const_made, 5)
            g.affine_select(out=ident[:, :], in_=ident[:, :], compare_op=ALU.not_equal, fill=1.0, base=0,
                            pattern=[[-1, P]], channel_multiplier=1).then_inc(const_made, 1)
            g.affine_select(out=later[:, :], in_=ones[:, :], compare_op=ALU.is_gt, fill=0.0, base=0,
                            pattern=[[1, P]], channel_multiplier=-1).then_inc(const_made, 1)

            def split_lo(u, j):
                pool.wait_ge(hi_split, u + 1)
                s = slice(j * UNIT, (j + 1) * UNIT)
                g.tensor_tensor(w_lo[:, s], raw[:, s], w_hi[:, s], ALU.subtract).then_inc(lo_split, 1)

            with pool.Fori(0, U_WO // RING + 1) as i:
                for j in range(RING):
                    split_lo(i * RING + j, j)
            for h in range(H):
                b = h % 2
                pool.wait_ge(rsum, h + 1)
                for t in range(NT):
                    s = slice((b * NT + t) * N, (b * NT + t + 1) * N)
                    r = sm[:, 12 * b + 9 + t:12 * b + 10 + t]
                    g.tensor_scalar(prob[:, s], prob[:, s], r, None, ALU.mult).then_inc(prob_ready, 1)
            with pool.Fori(U_WO // RING + 1, U_ROOT // RING) as i:
                for j in range(RING):
                    split_lo(i * RING + j, j)
            for j in range(RING):
                split_lo(U_ROOT + j, j)

            def inv_std(n):
                pool.wait_ge(var_made, n + 1)
                t = n % NT
                g.tensor_tensor(rstd[:, t:t + 1], vare[:, t:t + 1], nhalf[:, t:t + 1],
                                ALU.pow).then_inc(rstd_made, 1)

            for t in range(NT):
                inv_std(t)
            with pool.Fori(U_ROOT // RING + 1, UNITS // RING) as i:
                for j in range(RING):
                    split_lo(i * RING + j, j)
            for t in range(NT):
                inv_std(NT + t)

        @block.scalar
        def _(act):
            a = nc.scalar

            def split_hi(u, j, i):
                act.wait_ge(raw_loaded[j], 16 * (i + 1))
                s = slice(j * UNIT, (j + 1) * UNIT)
                a.activation(w_hi[:, s], raw[:, s], ACT.Copy).then_inc(hi_split, 1)

            def split_unit(u):
                if u < UNITS:
                    if u >= RING:
                        act.wait_ge(unit_done, u - RING + 1)
                    split_hi(u, u % RING, u // RING)

            act.wait_ge(x_loaded, 16)
            for c in range(2):
                s = slice(c * ACTS // 2, (c + 1) * ACTS // 2)
                a.activation(xt_hi[:, s], xt_raw[:, s], ACT.Copy).then_inc(x_hi, 1)
                if c == 0:
                    split_unit(0)
            for u in range(1, RING):
                split_unit(u)
            act.wait_ge(tw_dve, 1)
            a.activation(tw2[:, :], tw2[:, :], ACT.Exp).then_inc(tw_act, 1)
            act.wait_ge(tw_dve, 2)
            a.activation(tw2[:, :], tw2[:, :], ACT.Ln).then_inc(tw_act, 1)

            def split_next(first_round, j):
                act.wait_ge(raw_loaded[j % RING], (first_round + j // RING + 2) * 16)
                s = slice(j % RING * UNIT, (j % RING + 1) * UNIT)
                a.activation(w_hi[:, s], raw[:, s], ACT.Copy).then_inc(hi_split, 1)

            with act.Fori(0, 3) as i:
                for j in range(KT):
                    u = i * KT + j
                    act.wait_ge(unit_done, u + 1)
                    a.activation(t1_hi[:, bass.ds(u * N, N)], bank[j % RING][:, 0:N], ACT.Identity,
                                 bias=bias_col[:, bass.ds(u, 1)]).then_inc(f_hi, 1)
                    split_next(i * 2, j)
            with act.Fori(0, 2) as i:
                for j in range(KT):
                    u = i * KT + j
                    act.wait_ge(unit_done, u + U_F2 + 1)
                    a.activation(t2_hi[:, bass.ds(u * N, N)], bank[j % RING][:, 0:N], ACT.Identity,
                                 bias=bias_col[:, bass.ds(u + U_F2, 1)]).then_inc(f_hi, 1)
                    split_next(i * 2 + U_F2 // RING, j)
            for j in range(KT):
                u = U_F2 + 2 * KT + j
                act.wait_ge(unit_done, u + 1)
                if j == 0:
                    act.wait_ge(mask_made, 1)
                a.activation(v2t[:, j * N:(j + 1) * N], bank[j % RING][:, 0:N], ACT.Identity,
                             bias=bias_col[:, u:u + 1]).then_inc(v_ev, 1)
                split_unit(u + RING)
            for n in range(2 * NT):
                act.wait_ge(v_turned, n + 1)
                a.activation(v2_hi[:, n * HALF:(n + 1) * HALF], bank[4 + n % 4][:, :],
                             ACT.Copy).then_inc(v_hi, 1)

            def softmax(h):
                b = h % 2
                act.wait_ge(negmax, h + 1)
                if h >= 2:
                    act.wait_ge(p_turned, NT * (h - 1))
                for t in range(NT):
                    s = slice((b * NT + t) * N, (b * NT + t + 1) * N)
                    a.activation(prob[:, s], logit[:, s], ACT.Exp, scale=SCORE_SCALE,
                                 bias=sm[:, 12 * b + 3 + t:12 * b + 4 + t],
                                 accum_out=sm[:, 12 * b + 6 + t:12 * b + 7 + t]).then_inc(exp_done, 1)

            def take_pt(h):
                b = h % 2
                for m in range(NT):
                    act.wait_ge(p_turned, NT * h + m + 1)
                    if h >= 2 and m == 0:
                        act.wait_ge(pv_done, h - 1)
                    s = slice((b * NT + m) * N, (b * NT + m + 1) * N)
                    a.activation(pt_hi[:, s], bank[4 + m][:, 0:N], ACT.Copy).then_inc(pt_hi_made, 1)

            def take_o(h):
                act.wait_ge(pv_done, h + 1)
                q = slice(DH * (h % 2), DH * (h % 2) + DH)
                s = slice(h // 2 * N, (h // 2 + 1) * N)
                a.activation(o_hi[q, s], bank[7][q, 0:N], ACT.Copy).then_inc(o_hi_made, 1)

            for h in range(H + 1):
                if h < H:
                    softmax(h)
                if h >= 1:
                    take_pt(h - 1)
                    take_o(h - 1)

            for n in range(2 * 4):
                act.wait_ge(oh_used, OH + used_after(n))
                for t in range(NT):
                    m = n * NT + t
                    if m >= 2:
                        act.wait_ge(hist_decoded, m - 1)
                    a.activation(both_i[:, (m % 2) * N:(m % 2 + 1) * N], bank[(n % 2) * NT + t][:, 0:N],
                                 ACT.Copy).then_inc(hist_cast, 1)

            for u in range(U_WO + RING, U_ROOT + RING):
                split_unit(u)
            for k in range(KT):
                act.wait_ge(x1_turned, k + 1)
                a.activation(x1t_hi[:, k * N:(k + 1) * N], bank[6 + k % 2][:, 0:N],
                             ACT.Copy).then_inc(x1t_hi_made, 1)
            for r in range(R):
                if U_ROOT + RING + r < U_REL + RING:
                    split_unit(U_ROOT + RING + r)
                act.wait_ge(a_norm, r + 1)
                s = slice(r * NT * N, (r + 1) * NT * N)
                a.activation(a_hi[:, s], a_cnt[:, s], ACT.Copy).then_inc(a_hi_made, 1)
            act.wait_ge(a_ready, R)
            a.activation(x1h_hi[:, :], x1[:, :], ACT.Copy).then_inc(x1h_hi_made, 1)

            def take_mean(n, k):
                act.wait_ge(agg_done, n + 1)
                act.wait_ge(unit_done, n + (U_REL - 1))
                b = k % 2
                a.activation(mean_hi[:, b * N:(b + 1) * N], bank[6 + b][:, 0:N],
                             ACT.Copy).then_inc(mean_hi_made, 1)

            with act.Fori(0, R) as r:
                for k in range(KT):
                    n = r * KT + k
                    take_mean(n, k)
                    act.wait_ge(unit_done, n + (U_REL + 1))
                    split_next(r * 2 + U_REL // RING, k)
            for k in range(KT):
                act.wait_ge(u_turned, k + 1)
                a.activation(ut_hi[:, k * N:(k + 1) * N], bank[6 + k % 2][:, 0:N],
                             ACT.Copy).then_inc(ut_hi_made, 1)
            for t in range(NT):
                s = slice(t * D, (t + 1) * D)
                a.activation(gated[:, s], u_nat[:, s], ACT.Tanh).then_inc(tanh_made, 1)
                split_unit(U_GX + RING + t)
            for u in range(U_GX + RING + NT, UNITS):
                split_unit(u)

        @block.vector
        def _(v):
            d = nc.vector
            chained = [0]

            def after(ins):
                chained[0] += 1
                ins.then_inc(dve, 1)
                v.wait_ge(dve, chained[0])

            d.memset(dup_junk[:, :], 0.0).then_inc(f_lo, RING)
            d.memset(sm[:, :], 0.0).then_inc(oh_used, OH)
            d.memset(rstd[:, :], 0.0).then_inc(mean_ready, 1)
            for c in range(2):
                s = slice(c * ACTS // 2, (c + 1) * ACTS // 2)
                v.wait_ge(x_hi, c + 1)
                d.tensor_tensor(xt_lo[:, s], xt_raw[:, s], xt_hi[:, s], ALU.subtract).then_inc(x_ready, 1)

            v.wait_ge(small_loaded, 48)
            v.wait_ge(const_made, 5)
            d.tensor_copy(iota16[:, :], iota_i[:, :]).then_inc(rows_cast, 1)
            d.tensor_copy(erow_f[:, 0:2 * P], erow_i[:, 0:2 * P]).then_inc(rows_cast, 1)
            d.tensor_copy(erow_f[:, 3 * P:4 * P], erow_i[:, 3 * P:4 * P]).then_inc(rows_cast, 1)
            after(d.tensor_scalar(erow_s[:, P:2 * P], erow_i[:, 2 * P:3 * P], 3, None, ALU.add))
            after(d.tensor_scalar(erow_s[:, 2 * P:3 * P], erow_s[:, P:2 * P], 3, None, ALU.bitwise_and))
            after(d.tensor_tensor(erow_s[:, P:2 * P], erow_s[:, 2 * P:3 * P], erow_s[:, 0:P], ALU.add))
            d.tensor_scalar(erow_f[:, 2 * P:3 * P].bitcast(I32), erow_s[:, P:2 * P], 23, None,
                            ALU.logical_shift_left).then_inc(rows_cast, 1)
            after(d.tensor_scalar(tw3[:, :], tw[:, :], -1.0, None, ALU.mult))
            d.tensor_tensor(tw2[:, :], tw[:, :], tw3[:, :], ALU.min).then_inc(tw_dve, 1)
            v.wait_ge(tw_act, 1)
            d.tensor_scalar(tw2[:, :], tw2[:, :], 1.0, None, ALU.add).then_inc(tw_dve, 1)
            v.wait_ge(tw_act, 2)
            v.wait_ge(tw_dve, 2)
            after(d.tensor_scalar(tw3[:, :], tw[:, :], 0.0, None, ALU.max))
            after(d.tensor_tensor(tw3[:, :], tw3[:, :], tw2[:, :], ALU.add))
            after(d.tensor_scalar(tw[:, :], tw3[:, :], 1.0 / SCORE_SCALE, None, ALU.mult))
            v.wait_ge(cols_turned, 4)
            after(d.tensor_copy(cols[:, :], bank[7][:, 0:4 * EC]))
            after(d.scalar_tensor_tensor(key_col[:, :], cols[:, C_SRC:C_SRC + EC], float(N),
                                         cols[:, C_DST:C_DST + EC], ALU.mult, ALU.add))
            for p in range(R // 2):
                a_ = w_rel[:, p * EC:(p + 1) * EC]
                rel = cols[:, C_REL:C_REL + EC]
                after(d.tensor_scalar(a_, rel, float(2 * p + 1), float(FIELD), ALU.is_equal, ALU.mult))
                after(d.scalar_tensor_tensor(a_, rel, float(2 * p), a_, ALU.is_equal, ALU.add))
            v.wait_ge(keys_loaded, 32)
            after(d.scalar_tensor_tensor(key_row[:, :], key_src[:, :], float(N), key_dst[:, :],
                                         ALU.mult, ALU.add))

            def find_later(c):
                d.scalar_tensor_tensor(dup_junk[:, :], key_row[:, bass.ds(c * P, P)],
                                       key_col[:, bass.ds(c, 1)], later[:, :],
                                       ALU.is_equal, ALU.mult, accum_out=dup[:, bass.ds(c, 1)])\
                 .then_inc(dve, 1)

            chained0 = chained[0]
            with v.Fori(0, 3) as i:
                for j in range(KT):
                    u = i * KT + j
                    v.wait_ge(f_hi, u + 1)
                    d.scalar_tensor_tensor(t1_lo[:, bass.ds(u * N, N)], bank[j % RING][:, 0:N],
                                           bias_col[:, bass.ds(u, 1)], t1_hi[:, bass.ds(u * N, N)],
                                           ALU.add, ALU.subtract).then_inc(f_lo, 1)
                    v.wait_ge(dve, u * 2 + chained0)
                    find_later(u * 2)
                    v.wait_ge(dve, u * 2 + (chained0 + 1))
                    find_later(u * 2 + 1)
            chained[0] += 2 * 3 * KT
            for c in range(2 * 3 * KT, EC):
                v.wait_ge(dve, chained[0])
                find_later(c)
                chained[0] += 1
            v.wait_ge(dve, chained[0])
            after(d.scalar_tensor_tensor(w_code[:, :], dup[:, :], 0.0, cols[:, C_CODE:C_CODE + EC],
                                         ALU.is_equal, ALU.mult))
            with v.Fori(0, 2) as i:
                for j in range(KT):
                    u = i * KT + j
                    v.wait_ge(f_hi, u + (U_F2 + 1))
                    d.scalar_tensor_tensor(t2_lo[:, bass.ds(u * N, N)], bank[j % RING][:, 0:N],
                                           bias_col[:, bass.ds(u + U_F2, 1)],
                                           t2_hi[:, bass.ds(u * N, N)],
                                           ALU.add, ALU.subtract).then_inc(f_lo, 1)

            def one_hots(c, n, slot, w, w_at):
                v.wait_ge(oh_used, n + 1)
                s = slice(slot * N, (slot + 1) * N)
                d.tensor_scalar(src_oh[:, s], iota16[:, :], cols[:, bass.ds(c + C_SRC, 1)], None,
                                ALU.is_equal).then_inc(oh_ready, 1)
                d.tensor_scalar(dst_oh[:, s], iota16[:, :], cols[:, bass.ds(c + C_DST, 1)],
                                w[:, bass.ds(c + w_at, 1)], ALU.is_equal, ALU.mult).then_inc(oh_ready, 1)

            with v.Fori(0, EC // OH) as i:
                for j in range(OH):
                    one_hots(i * OH + j, i * OH + j, j, w_code, 0)

            v.wait_ge(oh_used, OH + EC)
            for t in range(NT):
                s = slice(t * N, (t + 1) * N)
                after(d.tensor_scalar(m_code[:, s], bank[4 + t][:, 0:N].bitcast(I32), 23, None,
                                      ALU.logical_shift_right))
            for t in range(NT):
                q = m_code[:, t * N + t * P:t * N + (t + 1) * P]
                after(d.scalar_tensor_tensor(q, ident[:, :], 3.0, q, ALU.mult, ALU.max))
            after(d.tensor_scalar(m_kind[:, :], m_code[:, :], 3, None, ALU.bitwise_and))
            after(d.tensor_scalar(mask[:, :], m_code[:, :], 0.0, ABSENT, ALU.is_equal, ALU.mult))
            for kind in range(4):
                after(d.tensor_scalar(m_part[:, :], m_kind[:, :], float(kind), tw[:, kind:kind + 1],
                                      ALU.is_equal, ALU.mult))
                ins = d.tensor_tensor(mask[:, :], mask[:, :], m_part[:, :], ALU.add)
                if kind < 3:
                    after(ins)
                else:
                    ins.then_inc(mask_made, 1)
            v.wait_ge(mask_made, 1)
            for n in range(2 * NT):
                s = slice(n * HALF, (n + 1) * HALF)
                v.wait_ge(v_hi, n + 1)
                d.tensor_tensor(v2_lo[:, s], bank[4 + n % 4][:, :], v2_hi[:, s],
                                ALU.subtract).then_inc(v_ready, 1)

            def logits(h):
                b = h % 2
                if h >= 2:
                    v.wait_ge(exp_done, NT * (h - 1))
                for t in range(NT):
                    m = h * NT + t
                    v.wait_ge(score_done, m + 1)
                    d.tensor_tensor_reduce(logit[:, (b * NT + t) * N:(b * NT + t + 1) * N],
                                           bank[m % 4][:, 0:N], mask[:, t * N:(t + 1) * N],
                                           1.0, ABSENT * 10, ALU.add, ALU.max,
                                           sm[:, 12 * b + t:12 * b + t + 1]).then_inc(logit_made, 1)
                v.wait_ge(logit_made, NT * (h + 1))
                d.tensor_scalar(sm[:, 12 * b + 3:12 * b + 6], sm[:, 12 * b:12 * b + 3], -SCORE_SCALE, None,
                                ALU.mult).then_inc(negmax, 1)

            def sums(h):
                b = h % 2
                v.wait_ge(exp_done, NT * (h + 1))
                d.reciprocal(sm[:, 12 * b + 9:12 * b + 12], sm[:, 12 * b + 6:12 * b + 9]).then_inc(rsum, 1)

            def take_pt_lo(h):
                b = h % 2
                for m in range(NT):
                    v.wait_ge(pt_hi_made, NT * h + m + 1)
                    s = slice((b * NT + m) * N, (b * NT + m + 1) * N)
                    d.tensor_tensor(pt_lo[:, s], bank[4 + m][:, 0:N], pt_hi[:, s],
                                    ALU.subtract).then_inc(pt_ready, 1)

            def take_o_lo(h):
                v.wait_ge(o_hi_made, h + 1)
                q = slice(DH * (h % 2), DH * (h % 2) + DH)
                s = slice(h // 2 * N, (h // 2 + 1) * N)
                d.tensor_tensor(o_lo[q, s], bank[7][q, 0:N], o_hi[q, s], ALU.subtract).then_inc(o_ready, 1)

            for h in range(H + 1):
                if h < H:
                    logits(h)
                    sums(h)
                if h >= 1:
                    take_pt_lo(h - 1)
                    take_o_lo(h - 1)

            decoded = [0]

            def decode(n):
                half, p = divmod(n, 4)
                for t in range(NT):
                    m = n * NT + t
                    v.wait_ge(hist_cast, m + 1)
                    both = both_i[:, (m % 2) * N:(m % 2 + 1) * N]
                    d.tensor_scalar(low_i[:, :], both, FIELD - 1, None, ALU.bitwise_and)\
                     .then_inc(dve, 1)
                    d.tensor_scalar(high_i[:, :], both, FIELD_BITS, None, ALU.logical_shift_right)\
                     .then_inc(hist_decoded, 1)
                    chained[0] += 1
                    v.wait_ge(dve, chained[0])
                    v.wait_ge(hist_decoded, m + 1)
                    for r, part in ((2 * p, low_i), (2 * p + 1, high_i)):
                        q = a_cnt[:, (r * NT + t) * N:(r * NT + t + 1) * N]
                        if half == 0:
                            ins = d.tensor_copy(q, part[:, :])
                        else:
                            ins = d.tensor_tensor(q, q, part[:, :], ALU.add)
                        after(ins)

            used = EC
            for n in range(8):
                half, p = divmod(n, 4)
                c0, c1 = HALVES[half]
                with v.Fori(0, (c1 - c0) // OH) as i:
                    for j in range(OH):
                        one_hots(i * OH + (c0 + j), i * OH + (used + j), j, w_rel, p * EC)
                used += c1 - c0
                if n >= 1:
                    decode(n - 1)
            decode(7)
            d.tensor_copy(dup_junk[:, 0:1], sm[:, 0:1]).then_inc(cnt_made, 1)

            v.wait_ge(xres_loaded, 16)
            v.wait_ge(bo_loaded, 16)
            for t in range(NT):
                ins = d.tensor_tensor(x1[:, t * D:(t + 1) * D], x1[:, t * D:(t + 1) * D], row_bias[:, :],
                                      ALU.add)
                after(ins)
            d.tensor_copy(dup_junk[:, 0:1], sm[:, 0:1]).then_inc(xb_made, 1)

            def norm_stats(n, t, src):
                for half in range(2):
                    ins = d.bn_stats(stats[:, 12 * t + 6 * half:12 * t + 6 * half + 6],
                                     src[:, t * D + half * HALF:t * D + (half + 1) * HALF])
                    after(ins)
                after(d.bn_aggr(mv[:, 2 * t:2 * t + 2], stats[:, 12 * t:12 * t + 12]))
                d.tensor_scalar(vare[:, t:t + 1], mv[:, 2 * t + 1:2 * t + 2], EPS, None,
                                ALU.add).then_inc(var_made, 1)

            v.wait_ge(unit_done, U_ROOT)
            for t in range(NT):
                for half in range(2):
                    s = slice(t * D + half * HALF, t * D + (half + 1) * HALF)
                    ins = d.tensor_tensor(x1[:, s], bank[2 * t + half][:, :], x1[:, s], ALU.add)
                    ins.then_inc(res_made, 1)
                v.wait_ge(res_made, 2 * (t + 1))
                norm_stats(0, t, x1)
            for t in range(NT):
                v.wait_ge(rstd_made, t + 1)
                s = slice(t * D, (t + 1) * D)
                d.tensor_scalar(x1[:, s], x1[:, s], mv[:, 2 * t:2 * t + 1], rstd[:, t:t + 1],
                                ALU.subtract, ALU.mult).then_inc(x1_made, 1)
            for k in range(KT):
                v.wait_ge(x1t_hi_made, k + 1)
                s = slice(k * N, (k + 1) * N)
                d.tensor_tensor(x1t_lo[:, s], bank[6 + k % 2][:, 0:N], x1t_hi[:, s],
                                ALU.subtract).then_inc(x1t_ready, 1)

            def normalise(r):
                rc = rcount[:, (r % 2) * N:(r % 2 + 1) * N]
                v.wait_ge(cnt_summed, r + 1)
                after(d.tensor_scalar(rc, bank[6 + r % 2][:, 0:N], 1.0, None, ALU.max))
                after(d.reciprocal(rc, rc))
                for t in range(NT):
                    q = a_cnt[:, (r * NT + t) * N:(r * NT + t + 1) * N]
                    ins = d.tensor_tensor(q, q, rc, ALU.mult)
                    if t < NT - 1:
                        after(ins)
                    else:
                        ins.then_inc(a_norm, 1)

            def split_a(r):
                s = slice(r * NT * N, (r + 1) * NT * N)
                v.wait_ge(a_hi_made, r + 1)
                d.tensor_tensor(a_lo[:, s], a_cnt[:, s], a_hi[:, s], ALU.subtract).then_inc(a_ready, 1)

            for r in range(R):
                normalise(r)
                if r >= 1:
                    split_a(r - 1)
            split_a(R - 1)
            v.wait_ge(x1h_hi_made, 1)
            d.tensor_tensor(x1h_lo[:, :], x1[:, :], x1h_hi[:, :], ALU.subtract).then_inc(x1h_ready, 1)

            with v.Fori(0, R) as r:
                for k in range(KT):
                    v.wait_ge(mean_hi_made, r * KT + (k + 1))
                    b = k % 2
                    d.tensor_tensor(mean_lo[:, b * N:(b + 1) * N], bank[6 + b][:, 0:N],
                                    mean_hi[:, b * N:(b + 1) * N], ALU.subtract).then_inc(mean_ready, 1)
            v.wait_ge(rb_loaded, 16)
            v.wait_ge(unit_done, U_GX)
            for n in range(2 * NT):
                s = slice(n * HALF, (n + 1) * HALF)
                d.tensor_tensor(u_nat[:, s], bank[n][:, :], row_bias[:, (n % 2) * HALF:(n % 2 + 1) * HALF],
                                ALU.add).then_inc(u_made, 1)
            for k in range(KT):
                v.wait_ge(ut_hi_made, k + 1)
                s = slice(k * N, (k + 1) * N)
                d.tensor_tensor(ut_lo[:, s], bank[6 + k % 2][:, 0:N], ut_hi[:, s],
                                ALU.subtract).then_inc(ut_ready, 1)
            v.wait_ge(bg_loaded, 16)
            for t in range(NT):
                s = slice(t * D, (t + 1) * D)
                v.wait_ge(tanh_made, t + 1)
                after(d.tensor_tensor(gated[:, s], gated[:, s], x1[:, s], ALU.subtract))
                after(d.tensor_tensor(fixed[:, s], gated[:, s], row_bias[:, :], ALU.mult))
                after(d.scalar_tensor_tensor(fixed[:, s], x1[:, s], 2.0, fixed[:, s], ALU.mult, ALU.add))
            for t in range(NT):
                v.wait_ge(z_summed, t + 1)
                for half in range(2):
                    s = slice(t * D + half * HALF, t * D + (half + 1) * HALF)
                    after(d.tensor_tensor(result[:, s], bank[2 * t + half][:, :], gated[:, s], ALU.mult))
                s = slice(t * D, (t + 1) * D)
                after(d.tensor_tensor(result[:, s], result[:, s], fixed[:, s], ALU.add))
                norm_stats(NT, t, result)
                v.wait_ge(rstd_made, NT + t + 1)
                d.tensor_scalar(result[:, s], result[:, s], mv[:, 2 * t:2 * t + 1], rstd[:, t:t + 1],
                                ALU.subtract, ALU.mult).then_inc(out_made, 1)

        @block.tensor
        def _(pe):
            mm = nc.tensor.matmul

            def three(dst, l_hi, l_lo, r_hi, r_lo, start, stop):
                mm(dst, l_hi, r_hi, start=start, stop=False)
                mm(dst, l_hi, r_lo, start=False, stop=False)
                return mm(dst, l_lo, r_hi, start=False, stop=stop)

            pe.wait_ge(x_ready, 2)

            def f_unit(u, j, src_hi, src_lo, at):
                pe.wait_ge(lo_split, u + 1)
                for k in range(KT):
                    w = slice((j % RING) * UNIT + k * P, (j % RING) * UNIT + (k + 1) * P)
                    m = bass.ds(at + k * N, N)
                    last = three(bank[j % RING][:, 0:N], w_hi[:, w], w_lo[:, w], src_hi[:, m], src_lo[:, m],
                                 k == 0, k == KT - 1)
                last.then_inc(unit_done, 1)

            pe.wait_ge(f_lo, 1)
            f_unit(0, 0, xt_hi, xt_lo, 0)
            pe.wait_ge(rows_cast, 4)
            pe.wait_ge(const_made, 7)
            for n in range(4):
                nc.tensor.transpose(bank[7][:, n * EC:(n + 1) * EC], erow_f[:, n * P:(n + 1) * P],
                                    ident[0:EC, 0:EC]).then_inc(cols_turned, 1)
            for j in range(1, KT):
                pe.wait_ge(f_lo, j + 1)
                f_unit(j, j, xt_hi, xt_lo, 0)
            with pe.Fori(1, 3) as i:
                for j in range(KT):
                    pe.wait_ge(f_lo, i * KT + (j + 1))
                    f_unit(i * KT + j, j, xt_hi, xt_lo, 0)
            pe.wait_ge(f_lo, U_F2 + RING - KT)
            with pe.Fori(0, 2) as i:
                for j in range(KT):
                    pe.wait_ge(f_lo, i * KT + (U_F2 + j + 1))
                    f_unit(i * KT + (U_F2 + j), j, t1_hi, t1_lo, i * ACTS)

            def histogram(c0, c1, used, banks):
                def chunk(n, slot, start, stop):
                    pe.wait_ge(oh_ready, (n + 1) * 2)
                    m = slice(slot * N, (slot + 1) * N)
                    for t in range(NT):
                        last = mm(bank[banks[t]][:, 0:N], src_oh[:, slot * N + t * P:slot * N + (t + 1) * P],
                                  dst_oh[:, m], start=start, stop=stop)
                    last.then_inc(oh_used, 1)
                    return last
                for j in range(OH):
                    chunk(used + j, j, j == 0, False)
                with pe.Fori(1, (c1 - c0) // OH - 1) as i:
                    for j in range(OH):
                        chunk(i * OH + (used + j), j, False, False)
                for j in range(OH):
                    chunk(used + c1 - c0 - OH + j, j, False, j == OH - 1)

            histogram(0, EC, 0, (4, 5, 6))
            pe.wait_ge(f_lo, U_F2 + 2 * KT + RING)
            for j in range(KT):
                if j >= RING:
                    pe.wait_ge(v_ev, j - RING + 1)
                f_unit(U_F2 + 2 * KT + j, j, t1_hi, t1_lo, 2 * ACTS)
            pe.wait_ge(v_ev, KT)
            pe.wait_ge(mask_made, 1)
            for n in range(2 * NT):
                t, half = divmod(n, 2)
                if n >= 4:
                    pe.wait_ge(v_ready, n - 3)
                for q in range(4):
                    o = half * 4 + q
                    last = nc.tensor.transpose(bank[4 + n % 4][:, q * P:(q + 1) * P],
                                               v2t[:, o * N + t * P:o * N + (t + 1) * P], ident[:, :])
                last.then_inc(v_turned, 1)
            pe.wait_ge(v_ready, 2 * NT)

            def scores(h):
                q = slice(DH * (h % 2), DH * (h % 2) + DH)
                for t in range(NT):
                    m = h * NT + t
                    if m >= 4:
                        pe.wait_ge(logit_made, m - 3)
                    n0 = h // 2 * N
                    sq = slice(n0 + t * P, n0 + (t + 1) * P)
                    sk = slice(ACTS + n0, ACTS + n0 + N)
                    three(bank[m % 4][:, 0:N], t2_hi[q, sq], t2_lo[q, sq], t2_hi[q, sk], t2_lo[q, sk],
                          True, True).then_inc(score_done, 1)

            def turn_p(h):
                b = h % 2
                for m in range(NT):
                    if h >= 1:
                        pe.wait_ge(pt_ready, NT * (h - 1) + m + 1)
                    for t in range(NT):
                        pe.wait_ge(prob_ready, NT * h + t + 1)
                        s0 = (b * NT + t) * N + m * P
                        last = nc.tensor.transpose(bank[4 + m][:, t * P:(t + 1) * P],
                                                   prob[:, s0:s0 + P], ident[:, :])
                    last.then_inc(p_turned, 1)

            def weigh_v(h):
                b = h % 2
                if h >= 1:
                    pe.wait_ge(o_ready, h)
                for m in range(NT):
                    pe.wait_ge(pt_ready, NT * h + m + 1)
                    sv = slice(m * D + h // 2 * P, m * D + (h // 2 + 1) * P)
                    s = slice((b * NT + m) * N, (b * NT + m + 1) * N)
                    last = three(bank[7][:, 0:N], v2_hi[:, sv], v2_lo[:, sv], pt_hi[:, s], pt_lo[:, s],
                                 m == 0, m == NT - 1)
                last.then_inc(pv_done, 1)

            for h in range(H + 1):
                if h < H:
                    scores(h)
                if h >= 1:
                    turn_p(h - 1)
                    weigh_v(h - 1)

            used = EC
            pe.wait_ge(logit_made, NT * H)
            pe.wait_ge(pt_ready, NT * H)
            for n in range(8):
                c0, c1 = HALVES[n // 4]
                if n >= 2:
                    pe.wait_ge(hist_cast, NT * (n - 1))
                histogram(c0, c1, used, tuple((n % 2) * NT + t for t in range(NT)))
                used += c1 - c0

            def n_unit(u, l_hi, l_lo, at, step, start, stop, wait_bank=None):
                pe.wait_ge(lo_split, u + 1)
                w0 = (u % RING) * UNIT if isinstance(u, int) else None
                return n_body(w0, l_hi, l_lo, at, start, stop, wait_bank)

            def n_body(w0, l_hi, l_lo, at, start, stop, wait_bank=None, each=None):
                for t in range(NT):
                    if wait_bank:
                        wait_bank(t)
                    s = slice(at + t * P, at + (t + 1) * P)
                    for half in range(2):
                        w = slice(w0 + half * HALF, w0 + (half + 1) * HALF)
                        last = three(bank[2 * t + half][:, :], l_hi[:, s], l_lo[:, s], w_hi[:, w],
                                     w_lo[:, w], start, stop)
                    if each is not None and t < NT - 1:
                        last.then_inc(each, 1)
                return last

            pe.wait_ge(o_ready, H)
            pe.wait_ge(hist_cast, NT * 8)
            for k in range(KT):
                n_unit(U_WO + k, o_hi, o_lo, k * N, 0, k == 0, k == KT - 1).then_inc(unit_done, 1)
            pe.wait_ge(x1_made, NT)
            for k in range(KT):
                if k >= 2:
                    pe.wait_ge(x1t_ready, k - 1)
                for t in range(NT):
                    last = nc.tensor.transpose(bank[6 + k % 2][:, t * P:(t + 1) * P],
                                               x1[:, t * D + k * P:t * D + (k + 1) * P], ident[:, :])
                last.then_inc(x1_turned, 1)
            pe.wait_ge(cnt_made, 1)

            def count(r):
                if r >= 2:
                    pe.wait_ge(a_norm, r - 1)
                for t in range(NT):
                    last = mm(bank[6 + r % 2][:, 0:N], ones[:, :],
                              a_cnt[:, (r * NT + t) * N:(r * NT + t + 1) * N], start=t == 0, stop=t == NT - 1)
                last.then_inc(cnt_summed, 1)

            pe.wait_ge(x1t_ready, KT)
            count(0)
            count(1)
            for k in range(KT):
                n_unit(U_ROOT + k, x1t_hi, x1t_lo, k * N, 0, k == 0, False).then_inc(unit_done, 1)
                if k + 2 < R:
                    count(k + 2)
            pe.wait_ge(x1h_ready, 1)

            def aggregate(n, k, at):
                pe.wait_ge(mean_ready, n)
                for s_ in range(NT):
                    s = slice(s_ * D + k * P, s_ * D + (k + 1) * P)
                    m = bass.ds(at + s_ * N, N)
                    last = three(bank[6 + k % 2][:, 0:N], x1h_hi[:, s], x1h_lo[:, s], a_hi[:, m], a_lo[:, m],
                                 s_ == 0, s_ == NT - 1)
                last.then_inc(agg_done, 1)

            def weigh_mean(n, k, stop):
                pe.wait_ge(mean_ready, n + 2)
                pe.wait_ge(lo_split, n + (U_REL + 1))
                n_body((k % RING) * UNIT, mean_hi, mean_lo, (k % 2) * N, False, stop).then_inc(unit_done, 1)

            def first_aggregate():
                for s_ in range(NT):
                    last = three(bank[6][:, 0:N], x1h_hi[:, s_ * D:s_ * D + P], x1h_lo[:, s_ * D:s_ * D + P],
                                 a_hi[:, s_ * N:(s_ + 1) * N], a_lo[:, s_ * N:(s_ + 1) * N],
                                 s_ == 0, s_ == NT - 1)
                last.then_inc(agg_done, 1)

            first_aggregate()
            with pe.Fori(0, R - 1) as r:
                for k in range(KT):
                    n = r * KT + k
                    aggregate(n + 1, (k + 1) % KT, (r + (1 if k == KT - 1 else 0)) * (NT * N))
                    weigh_mean(n, k, False)
            for k in range(KT):
                n = (R - 1) * KT + k
                if k < KT - 1:
                    aggregate(n + 1, k + 1, (R - 1) * NT * N)
                weigh_mean(n, k, k == KT - 1)

            for k in range(KT):
                n_unit(U_GX + k, x1t_hi, x1t_lo, k * N, 0, k == 0, False,
                       (lambda t: pe.wait_ge(u_made, 2 * t + 2)) if k == 0 else None).then_inc(unit_done, 1)
                if k == 0:
                    for kk in range(KT):
                        if kk >= 2:
                            pe.wait_ge(ut_ready, kk - 1)
                        for t in range(NT):
                            last = nc.tensor.transpose(
                                bank[6 + kk % 2][:, t * P:(t + 1) * P],
                                u_nat[:, t * D + kk * P:t * D + (kk + 1) * P], ident[:, :])
                        last.then_inc(u_turned, 1)
            pe.wait_ge(ut_ready, KT)
            for k in range(KT):
                pe.wait_ge(lo_split, U_GU + k + 1)
                last = n_body((k % RING) * UNIT, ut_hi, ut_lo, k * N, False, k == KT - 1, None,
                              z_summed if k == KT - 1 else None)
                last.then_inc(unit_done if k < KT - 1 else z_summed, 1)


def kernel(**inputs):
    import numpy as np
    import concourse.bacc as bacc
    from concourse.bass_utils import run_bass_kernel_spmd as run

    i = {k: np.asarray(v) for k, v in inputs.items()}
    p, n, d = 128, 384, 1024
    kt, nt = d // p, n // p
    e = i["src"].shape[0]

    def f_order(w):
        return w.reshape(kt, p, kt, p).transpose(0, 3, 2, 1).reshape(kt, p, d)

    def n_order(w):
        return w.reshape(kt, p, d)

    g = {k[7:]: v for k, v in i.items() if k.startswith("L")}
    weights = np.concatenate(
        [f_order(g[k]) for k in ("wq", "wk", "wv", "wiq", "wik", "wiv")]
        + [n_order(g["wo"].T), n_order(g["root"])]
        + [n_order(w) for w in g["weight"]]
        + [n_order(g["w_gate"][d:]), n_order(g["w_gate"][:d])])
    arrays = {
        "x_nat": i["x"].reshape(nt, p, d).transpose(1, 0, 2).reshape(p, nt * d),
        "x_t": i["x"].T.reshape(kt, p, n).transpose(1, 0, 2).reshape(p, kt * n),
        "edges": np.concatenate([i[k].reshape(e // p, p) for k in ("src", "dst", "edge_type_5", "edge_type_8")], 1),
        "keys_src": i["src"], "keys_dst": i["dst"],
        "type_w": g["edge_type_weights"],
        "bias_f": np.concatenate([g[k].reshape(kt, p) for k in ("bq", "bk", "bv", "biq", "bik", "biv")]).T,
        "bo": g["bo"], "bias": g["bias"], "b_gate": g["b_gate"],
        "weights": weights,
    }
    arrays = {k: np.ascontiguousarray(v) for k, v in arrays.items()}
    nc = bacc.Bacc("TRN2", target_bir_lowering=False, num_devices=1)
    args = [nc.dram_tensor(k, v.shape, mybir.dt.from_np(v.dtype), kind="ExternalInput").ap()
            for k, v in arrays.items()]
    out = nc.dram_tensor("out_dram", (nt, p, d), mybir.dt.float32, kind="ExternalOutput").ap()
    build(nc, *args, out)
    r = run(nc, [arrays], core_ids=[0])
    return np.asarray(r.results[0]["out_dram"]).reshape(n, d)
```

```python
import concourse.bass as bass
from concourse import mybir
from contextlib import ExitStack

F32 = mybir.dt.float32
F32R = mybir.dt.float32r
BF16 = mybir.dt.bfloat16
F16 = mybir.dt.float16
I32 = mybir.dt.int32
ALU = mybir.AluOpType
ACT = mybir.ActivationFunctionType
AX = mybir.AxisListType

P = 128
N = 384
NT = N // P
D = 1024
KT = D // P
H = 16
DH = D // H
E = 6528
EC = E // P
R = 8
EPS = 1e-5
HALF = 512

UNIT = KT * P
RING = 4
U_F1 = 0
U_F2 = 3 * KT
U_WO = 6 * KT
U_ROOT = 7 * KT
U_REL = 8 * KT
U_GX = U_REL + R * KT
U_GU = U_GX + KT
UNITS = U_GU + KT

XC = 4
OH = 3
DIGIT_BITS = 3
DIGIT_LIMIT = float(2 ** (DIGIT_BITS * R))
HALVES = ((0, 27), (27, EC))
FIELD = 4096
FIELD_BITS = 12
ABSENT = -1e30
SCORE_SCALE = 1.0 / (DH ** 0.5)


def build(nc, x_nat, x_t, edges, keys_src, keys_dst, type_w, bias_f, bo, bias, b_gate, weights, out):
    ctx = ExitStack()
    with ctx:
        base = nc.sbuf_base
        base = (base + 31) // 32 * 32
        place = [base]

        def region(size):
            at = place[0]
            place[0] += (size + 31) // 32 * 32
            return at

        def sb(name, cols, dt, at=None, parts=P):
            size = cols * (2 if dt in (BF16, F16) else 4)
            if at is None:
                at = region(size)
            return nc.alloc_sbuf_tensor_at(name, [parts, cols], dt, offset=at)

        raw = sb("raw", RING * UNIT, F32)
        w_hi = sb("w_hi", RING * UNIT, F32R)
        w_lo = sb("w_lo", RING * UNIT, F32R)

        ACTS = KT * N
        z1 = region(2 * 3 * ACTS * 4)
        z1b = z1 + 3 * ACTS * 4
        z2 = region(4 * ACTS * 4)
        onehots = region(2 * OH * N * 2)
        z3 = region(2 * ACTS * 4)

        t1_hi = sb("t1_hi", 3 * ACTS, F32R, z1)
        t1_lo = sb("t1_lo", 3 * ACTS, F32R, z1b)
        erow_at = z1b + (3 * ACTS - 16 * P) * 4
        erow_i = sb("erow_i", 4 * P, I32, erow_at, EC)
        erow_f = sb("erow_f", 4 * P, F32, erow_at + 4 * P * 4, EC)
        erow_s = sb("erow_s", 3 * P, I32, erow_at + 8 * P * 4, EC)
        v2t = sb("v2t", ACTS, F32, z1)
        logit = sb("logit", 2 * NT * N, F32, z1)
        prob = [sb(f"prob{i}", NT * N, F32, at) for i, at in
                enumerate((z1 + 2 * NT * N * 4, z1 + 3 * NT * N * 4, z1b))]
        pt_hi = sb("pt_hi", 2 * NT * N, F32R, z1 + 4 * NT * N * 4)
        pt_lo = sb("pt_lo", 2 * NT * N, F32R, z1 + 6 * NT * N * 4)
        o_hi = sb("o_hi", ACTS, F32R, z1b + ACTS * 4)
        o_lo = sb("o_lo", ACTS, F32R, z1b + 2 * ACTS * 4)
        a_hi = sb("a_hi", R * NT * N, F32R, z1)
        a_lo = sb("a_lo", R * NT * N, F32R, z1b)
        u_nat = sb("u_nat", ACTS, F32, z1)
        gated = sb("gated", ACTS, F32, z1 + ACTS * 4)
        fixed = sb("fixed", ACTS, F32, z1 + 2 * ACTS * 4)
        ut_hi = sb("ut_hi", ACTS, F32R, z1b)
        ut_lo = sb("ut_lo", ACTS, F32R, z1b + ACTS * 4)
        result = sb("result", ACTS, F32, z1b + 2 * ACTS * 4)

        digits = sb("digits", NT * N, I32, z1b + NT * N * 4)
        both_i = sb("both_i", 2 * N, I32, z1)
        low_i = sb("low_i", N, I32, z1 + 2 * N * 4)
        high_i = sb("high_i", N, I32, z1 + 3 * N * 4)

        key_src = sb("key_src", E, I32, z2)
        key_row = sb("key_row", E, F32, z2)
        key_dst = sb("key_dst", E, I32, z2 + E * 4)
        t2_hi = sb("t2_hi", 2 * ACTS, F32R, z2)
        t2_lo = sb("t2_lo", 2 * ACTS, F32R, z2 + 2 * ACTS * 4)
        a_cnt = sb("a_cnt", R * NT * N, F32, z2)
        x1h_hi = sb("x1h_hi", ACTS, F32R, z2)
        x1h_lo = sb("x1h_lo", ACTS, F32R, z2 + ACTS * 4)
        mean_hi = sb("mean_hi", 2 * N, F32R, z2 + 2 * ACTS * 4)
        mean_lo = sb("mean_lo", 2 * N, F32R, z2 + 2 * ACTS * 4 + 2 * N * 4)
        x1 = sb("x1", ACTS, F32, z2 + 3 * ACTS * 4)

        xt_hi = sb("xt_hi", ACTS, F32R, z3)
        xt_lo = sb("xt_lo", ACTS, F32R, z3 + ACTS * 4)
        v2_hi = sb("v2_hi", ACTS, F32R, z3)
        v2_lo = sb("v2_lo", ACTS, F32R, z3 + ACTS * 4)
        x1t_hi = sb("x1t_hi", ACTS, F32R, z3)
        x1t_lo = sb("x1t_lo", ACTS, F32R, z3 + ACTS * 4)
        rcount = sb("rcount", 2 * N, F32, onehots)
        one_digit = sb("one_digit", NT * N, I32, onehots)

        src_oh = sb("src_oh", OH * N, BF16, onehots)
        dst_oh = sb("dst_oh", OH * N, BF16, onehots + OH * N * 2)

        mask_at = region(NT * N * 4)
        mask = sb("mask", NT * N, F32, mask_at)
        row_bias = sb("row_bias", D, F32, mask_at)
        digits_raw = sb("digits_raw", NT * N, I32, mask_at)
        m_code = sb("m_code", NT * N, I32, z1b + 2 * NT * N * 4)
        m_kind = sb("m_kind", NT * N, I32, z1b + 3 * NT * N * 4)
        m_part = sb("m_part", NT * N, F32, z1b + 4 * NT * N * 4)

        xt_raw = sb("xt_raw", ACTS, F32, z1)

        iota_i = sb("iota_i", N, I32, mask_at)
        iota16 = sb("iota16", N, F16)
        ident = sb("ident", P, F32)
        ones = sb("ones", P, F32)
        later = sb("later", P, F32)
        cols = sb("cols", 4 * EC, F32)
        C_SRC, C_DST, C_CODE, C_REL = (i * EC for i in range(4))
        key_col = sb("key_col", EC, F32)
        dup = sb("dup", EC, F32)
        w_code = sb("w_code", EC, F32)
        w_digit = sb("w_digit", EC, I32)
        w_rel = sb("w_rel", 4 * EC, F32)
        digit_sum = sb("digit_sum", R * NT, F32)
        digit_total = sb("digit_total", 1, F32)
        counted = sb("counted", 1, I32)
        dup_junk = sb("dup_junk", P, F32)
        bias_col = sb("bias_col", 6 * KT, F32)
        tw = sb("tw", 4, F32)
        tw2 = sb("tw2", 4, F32)
        tw3 = sb("tw3", 4, F32)
        sm = sb("sm", 3 * 4 * NT, F32)
        stats = sb("stats", NT * 12, F32)
        mv = sb("mv", NT * 2, F32)
        rstd = sb("rstd", NT, F32)
        nhalf = sb("nhalf", NT, F32)
        vare = sb("vare", NT, F32)
        assert place[0] <= nc.sbuf_usable_end, (place[0], nc.sbuf_usable_end)

        bank = [ctx.enter_context(nc.psum_tensor(f"bank{i}", [P, HALF], F32)) for i in range(8)]

        def sem(name):
            return ctx.enter_context(nc.semaphore(name))

        raw_loaded = [sem(f"raw_loaded{j}") for j in range(RING)]
        hi_split = sem("hi_split")
        lo_split = sem("lo_split")
        unit_done = sem("unit_done")
        x_loaded = [sem(f"x_loaded{c}") for c in range(XC)]
        small_loaded = sem("small_loaded")
        keys_loaded = sem("keys_loaded")
        const_made = sem("const_made")
        x_hi = sem("x_hi")
        x_ready = sem("x_ready")
        f_hi = sem("f_hi")
        f_lo = sem("f_lo")
        v_ev = sem("v_ev")
        rows_cast = sem("rows_cast")
        cols_turned = sem("cols_turned")
        dve = sem("dve")
        oh_ready = sem("oh_ready")
        oh_used = sem("oh_used")
        digits_saved = sem("digits_saved")
        mask_read = sem("mask_read")
        digit_cut = sem("digit_cut")
        digit_taken = sem("digit_taken")
        total_made = sem("total_made")
        counted_made = sem("counted_made")
        general = sem("general")
        hist_cast = sem("hist_cast")
        hist_decoded = sem("hist_decoded")
        mask_made = sem("mask_made")
        tw_act = sem("tw_act")
        tw_dve = sem("tw_dve")
        v_turned = sem("v_turned")
        v_hi = sem("v_hi")
        v_ready = sem("v_ready")
        score_done = sem("score_done")
        logit_made = sem("logit_made")
        negmax = sem("negmax")
        exp_done = sem("exp_done")
        rsum = sem("rsum")
        prob_ready = sem("prob_ready")
        p_turned = sem("p_turned")
        pt_hi_made = sem("pt_hi_made")
        pt_ready = sem("pt_ready")
        pv_done = sem("pv_done")
        o_hi_made = sem("o_hi_made")
        o_ready = sem("o_ready")
        xres_loaded = sem("xres_loaded")
        bo_loaded = sem("bo_loaded")
        rb_loaded = sem("rb_loaded")
        bg_loaded = sem("bg_loaded")
        xb_made = sem("xb_made")
        res_made = sem("res_made")
        var_made = sem("var_made")
        rstd_made = sem("rstd_made")
        x1_made = sem("x1_made")
        x1_turned = sem("x1_turned")
        x1t_hi_made = sem("x1t_hi_made")
        x1t_ready = sem("x1t_ready")
        cnt_made = sem("cnt_made")
        cnt_summed = sem("cnt_summed")
        a_norm = sem("a_norm")
        a_hi_made = sem("a_hi_made")
        a_ready = sem("a_ready")
        x1h_hi_made = sem("x1h_hi_made")
        x1h_ready = sem("x1h_ready")
        agg_done = sem("agg_done")
        mean_hi_made = sem("mean_hi_made")
        mean_ready = sem("mean_ready")
        u_summed = sem("u_summed")
        u_made = sem("u_made")
        u_turned = sem("u_turned")
        ut_hi_made = sem("ut_hi_made")
        ut_ready = sem("ut_ready")
        tanh_made = sem("tanh_made")
        z_summed = sem("z_summed")
        out_made = sem("out_made")
        stored = sem("stored")

        CODE0 = 4

        def used_after(n):
            half, p = divmod(n, 4)
            return 2 * EC + 4 * sum(b - a for a, b in HALVES[:half]) + (p + 1) * (HALVES[half][1] - HALVES[half][0])

        MASK_TILE = 3
        DIGIT_STEPS = R * NT // 4

        block = ctx.enter_context(nc.Block())

        @block.sync
        def _(sp):
            for c in range(XC):
                s = slice(c * ACTS // XC, (c + 1) * ACTS // XC)
                sp.dma_start(xt_raw[:, s], x_t[:, s]).then_inc(x_loaded[c], 16)
                if c == 0:
                    sp.dma_start(raw[:, 0:UNIT], weights[0]).then_inc(raw_loaded[0], 16)
            for j in range(1, RING):
                sp.dma_start(raw[:, j * UNIT:(j + 1) * UNIT], weights[j]).then_inc(raw_loaded[j], 16)
            sp.dma_start(bias_col[:, :], bias_f).then_inc(small_loaded, 16)
            sp.dma_start(erow_i[:, :], edges).then_inc(small_loaded, 16)
            sp.dma_start(tw[:, :], type_w.partition_broadcast(P)).then_inc(small_loaded, 16)

            def load(u, j):
                sp.wait_ge(lo_split, u - RING + 1)
                sp.dma_start(raw[:, j * UNIT:(j + 1) * UNIT],
                             weights[bass.ds(u, 1)].rearrange("a p n -> (a p) n")).then_inc(raw_loaded[j], 16)

            for u in range(RING, KT):
                load(u, u % RING)
                for dst, src in ((key_src, keys_src), (key_dst, keys_dst)):
                    piece = slice((u - RING) * E // 4, (u - RING + 1) * E // 4)
                    sp.dma_start(dst[:, piece], src[piece].partition_broadcast(P)).then_inc(keys_loaded, 16)
            with sp.Fori(2, U_WO // RING + 1) as i:
                for j in range(RING):
                    load(i * RING + j, j)
            sp.wait_ge(score_done, H * NT)
            sp.dma_start(x1[:, :], x_nat).then_inc(xres_loaded, 16)
            sp.wait_ge(logit_made, H * NT)
            sp.dma_start(row_bias[:, :], bo.partition_broadcast(P)).then_inc(bo_loaded, 16)
            with sp.Fori(U_WO // RING + 1, U_REL // RING) as i:
                for j in range(RING):
                    load(i * RING + j, j)
            sp.wait_ge(xb_made, 1)
            sp.dma_start(row_bias[:, :], bias.partition_broadcast(P)).then_inc(rb_loaded, 16)
            with sp.Fori(U_REL // RING, UNITS // RING) as i:
                for j in range(RING):
                    load(i * RING + j, j)
            sp.wait_ge(u_made, 2 * NT)
            sp.dma_start(row_bias[:, :], b_gate.partition_broadcast(P)).then_inc(bg_loaded, 16)
            for t in range(NT):
                sp.wait_ge(out_made, t + 1)
                sp.dma_start(out[t], result[:, t * D:(t + 1) * D]).then_inc(stored, 16)
            sp.wait_ge(stored, 16 * NT)

        @block.gpsimd
        def _(pool):
            g = nc.gpsimd
            g.memset(ident[:, :], 0.0).then_inc(const_made, 1)
            g.memset(ones[:, :], 1.0).then_inc(const_made, 1)
            g.memset(nhalf[:, :], -0.5).then_inc(const_made, 1)
            g.iota(iota_i[:, :], pattern=[[1, N]], base=0, channel_multiplier=0).then_inc(const_made, 1)
            g.iota(erow_s[:, 0:P], pattern=[[0, P]], base=CODE0, channel_multiplier=4).then_inc(const_made, 1)
            pool.wait_ge(const_made, 5)
            g.affine_select(out=ident[:, :], in_=ident[:, :], compare_op=ALU.not_equal, fill=1.0, base=0,
                            pattern=[[-1, P]], channel_multiplier=1).then_inc(const_made, 1)
            g.affine_select(out=later[:, :], in_=ones[:, :], compare_op=ALU.is_gt, fill=0.0, base=0,
                            pattern=[[1, P]], channel_multiplier=-1).then_inc(const_made, 1)

            def split_lo(u, j):
                pool.wait_ge(hi_split, u + 1)
                s = slice(j * UNIT, (j + 1) * UNIT)
                g.tensor_tensor(w_lo[:, s], raw[:, s], w_hi[:, s], ALU.subtract).then_inc(lo_split, 1)

            with pool.Fori(0, U_WO // RING + 1) as i:
                for j in range(RING):
                    split_lo(i * RING + j, j)
            for h in range(H):
                b = h % 3
                pool.wait_ge(rsum, h + 1)
                for t in range(NT):
                    s = slice(t * N, (t + 1) * N)
                    r = sm[:, 12 * b + 9 + t:12 * b + 10 + t]
                    g.tensor_scalar(prob[b][:, s], prob[b][:, s], r, 1.0, ALU.mult, ALU.mult).then_inc(prob_ready, 1)
            with pool.Fori(U_WO // RING + 1, U_ROOT // RING) as i:
                for j in range(RING):
                    split_lo(i * RING + j, j)
            for j in range(RING):
                split_lo(U_ROOT + j, j)

            def inv_std(n):
                pool.wait_ge(var_made, n + 1)
                t = n % NT
                g.tensor_tensor(rstd[:, t:t + 1], vare[:, t:t + 1], nhalf[:, t:t + 1],
                                ALU.pow).then_inc(rstd_made, 1)

            for t in range(NT):
                inv_std(t)
            with pool.Fori(U_ROOT // RING + 1, UNITS // RING) as i:
                for j in range(RING):
                    split_lo(i * RING + j, j)
            for t in range(NT):
                inv_std(NT + t)

        @block.scalar
        def _(act):
            a = nc.scalar

            def split_hi(u, j, i):
                act.wait_ge(raw_loaded[j], 16 * (i + 1))
                s = slice(j * UNIT, (j + 1) * UNIT)
                a.activation(w_hi[:, s], raw[:, s], ACT.Copy).then_inc(hi_split, 1)

            def split_unit(u):
                if u < UNITS:
                    if u >= RING:
                        act.wait_ge(unit_done, u - RING + 1)
                    split_hi(u, u % RING, u // RING)

            for c in range(XC):
                s = slice(c * ACTS // XC, (c + 1) * ACTS // XC)
                act.wait_ge(x_loaded[c], 16)
                a.activation(xt_hi[:, s], xt_raw[:, s], ACT.Copy).then_inc(x_hi, 1)
                if c == 0:
                    split_unit(0)
            for u in range(1, RING):
                split_unit(u)
            act.wait_ge(tw_dve, 1)
            a.activation(tw2[:, :], tw2[:, :], ACT.Exp).then_inc(tw_act, 1)
            act.wait_ge(tw_dve, 2)
            a.activation(tw2[:, :], tw2[:, :], ACT.Ln).then_inc(tw_act, 1)

            def split_next(first_round, j, lead=0):
                act.wait_ge(raw_loaded[j % RING], (first_round + (j - lead) // RING + 2) * 16)
                s = slice(j % RING * UNIT, (j % RING + 1) * UNIT)
                a.activation(w_hi[:, s], raw[:, s], ACT.Copy).then_inc(hi_split, 1)

            with act.Fori(0, 3) as i:
                for j in range(KT):
                    u = i * KT + j
                    act.wait_ge(unit_done, u + 1)
                    a.activation(t1_hi[:, bass.ds(u * N, N)], bank[j % RING][:, 0:N], ACT.Identity,
                                 bias=bias_col[:, bass.ds(u, 1)]).then_inc(f_hi, 1)
                    split_next(i * 2, j)
            with act.Fori(0, 2) as i:
                for j in range(KT):
                    u = i * KT + j
                    act.wait_ge(unit_done, u + U_F2 + 1)
                    a.activation(t2_hi[:, bass.ds(u * N, N)], bank[j % RING][:, 0:N], ACT.Identity,
                                 bias=bias_col[:, bass.ds(u + U_F2, 1)]).then_inc(f_hi, 1)
                    split_next(i * 2 + U_F2 // RING, j)
            for j in range(KT):
                u = U_F2 + 2 * KT + j
                act.wait_ge(unit_done, u + 1)
                a.activation(v2t[:, j * N:(j + 1) * N], bank[j % RING][:, 0:N], ACT.Identity,
                             bias=bias_col[:, u:u + 1]).then_inc(v_ev, 1)
                split_unit(u + RING)
            for n in range(2 * NT):
                act.wait_ge(v_turned, n + 1)
                a.activation(v2_hi[:, n * HALF:(n + 1) * HALF], bank[4 + n % 4][:, :],
                             ACT.Copy).then_inc(v_hi, 1)

            def softmax(h):
                b = h % 3
                act.wait_ge(negmax, h + 1)
                if h >= 3:
                    act.wait_ge(p_turned, NT * (h - 2))
                for t in range(NT):
                    s = slice((h % 2 * NT + t) * N, (h % 2 * NT + t + 1) * N)
                    a.activation(prob[b][:, t * N:(t + 1) * N], logit[:, s], ACT.Exp, scale=SCORE_SCALE,
                                 bias=sm[:, 12 * b + 3 + t:12 * b + 4 + t],
                                 accum_out=sm[:, 12 * b + 6 + t:12 * b + 7 + t]).then_inc(exp_done, 1)

            def take_pt(h):
                b = h % 2
                for m in range(NT):
                    act.wait_ge(p_turned, NT * h + m + 1)
                    if h >= 2 and m == 0:
                        act.wait_ge(pv_done, h - 1)
                    s = slice((b * NT + m) * N, (b * NT + m + 1) * N)
                    a.activation(pt_hi[:, s], bank[4 + m][:, 0:N], ACT.Copy).then_inc(pt_hi_made, 1)

            def take_o(h):
                act.wait_ge(pv_done, h + 1)
                q = slice(DH * (h % 2), DH * (h % 2) + DH)
                s = slice(h // 2 * N, (h // 2 + 1) * N)
                a.activation(o_hi[q, s], bank[7][q, 0:N], ACT.Copy).then_inc(o_hi_made, 1)

            for i in range(H + 4):
                if 1 <= i <= H:
                    softmax(i - 1)
                if 3 <= i < H + 3:
                    take_pt(i - 3)
                if i >= 4:
                    take_o(i - 4)
                if i >= H:
                    for m in range((i - H) * DIGIT_STEPS, (i - H + 1) * DIGIT_STEPS):
                        act.wait_ge(digit_cut, m + 1)
                        a.activation(a_cnt[:, m * N:(m + 1) * N], one_digit[:, m % NT * N:(m % NT + 1) * N],
                                     ACT.Copy, accum_out=digit_sum[:, m:m + 1]).then_inc(digit_taken, 1)

            for u in range(U_WO + RING, U_ROOT + RING):
                split_unit(u)
            for k in range(KT):
                act.wait_ge(x1_turned, k + 1)
                a.activation(x1t_hi[:, k * N:(k + 1) * N], bank[6 + k % 2][:, 0:N],
                             ACT.Copy).then_inc(x1t_hi_made, 1)
            act.wait_ge(counted_made, 1)
            stands = act.value_load(counted[0:1, 0:1], min_val=0, max_val=1)
            with act.If(stands == 0):
                for n in range(2 * 4):
                    act.wait_ge(oh_used, OH + used_after(n))
                    for t in range(NT):
                        m = n * NT + t
                        if m >= 2:
                            act.wait_ge(hist_decoded, m - 1)
                        a.activation(both_i[:, (m % 2) * N:(m % 2 + 1) * N], bank[(n % 2) * NT + t][:, 0:N],
                                     ACT.Copy).then_inc(hist_cast, 1)
            for r in range(R):
                if U_ROOT + RING + r < U_REL + RING - 1:
                    split_unit(U_ROOT + RING + r)
                act.wait_ge(a_norm, r + 1)
                s = slice(r * NT * N, (r + 1) * NT * N)
                a.activation(a_hi[:, s], a_cnt[:, s], ACT.Copy).then_inc(a_hi_made, 1)
            act.wait_ge(a_ready, R)
            a.activation(x1h_hi[:, :], x1[:, :], ACT.Copy).then_inc(x1h_hi_made, 1)

            def take_mean(n, k):
                act.wait_ge(agg_done, n + 1)
                act.wait_ge(unit_done, n + (U_REL - 1))
                b = k % 2
                a.activation(mean_hi[:, b * N:(b + 1) * N], bank[6 + b][:, 0:N],
                             ACT.Copy).then_inc(mean_hi_made, 1)

            with act.Fori(0, R) as r:
                for k in range(KT):
                    n = r * KT + k
                    take_mean(n, k)
                    act.wait_ge(unit_done, n + U_REL)
                    split_next(r * 2 + U_REL // RING, k + RING - 1, RING)
            act.wait_ge(unit_done, U_GX)
            split_unit(U_GX + RING - 1)
            for k in range(KT):
                act.wait_ge(u_turned, k + 1)
                a.activation(ut_hi[:, k * N:(k + 1) * N], bank[6 + k % 2][:, 0:N],
                             ACT.Copy).then_inc(ut_hi_made, 1)
            for t in range(NT):
                s = slice(t * D, (t + 1) * D)
                a.activation(gated[:, s], u_nat[:, s], ACT.Tanh).then_inc(tanh_made, 1)
                split_unit(U_GX + RING + t)
            for u in range(U_GX + RING + NT, UNITS):
                split_unit(u)

        @block.vector
        def _(v):
            d = nc.vector
            chained = [0]

            def after(ins):
                chained[0] += 1
                ins.then_inc(dve, 1)
                v.wait_ge(dve, chained[0])

            d.memset(dup_junk[:, :], 0.0).then_inc(f_lo, RING)
            d.memset(sm[:, :], 0.0).then_inc(oh_used, OH)
            d.memset(rstd[:, :], 0.0).then_inc(mean_ready, 1)
            for c in range(XC):
                s = slice(c * ACTS // XC, (c + 1) * ACTS // XC)
                v.wait_ge(x_hi, c + 1)
                d.tensor_tensor(xt_lo[:, s], xt_raw[:, s], xt_hi[:, s], ALU.subtract).then_inc(x_ready, 1)

            v.wait_ge(small_loaded, 48)
            v.wait_ge(const_made, 5)
            d.tensor_copy(iota16[:, :], iota_i[:, :]).then_inc(rows_cast, 1)
            d.tensor_copy(erow_f[:, 0:2 * P], erow_i[:, 0:2 * P]).then_inc(rows_cast, 1)
            d.tensor_copy(erow_f[:, 3 * P:4 * P], erow_i[:, 3 * P:4 * P]).then_inc(rows_cast, 1)
            after(d.tensor_scalar(erow_s[:, P:2 * P], erow_i[:, 2 * P:3 * P], 3, None, ALU.add))
            after(d.tensor_scalar(erow_s[:, 2 * P:3 * P], erow_s[:, P:2 * P], 3, None, ALU.bitwise_and))
            after(d.tensor_tensor(erow_s[:, P:2 * P], erow_s[:, 2 * P:3 * P], erow_s[:, 0:P], ALU.add))
            d.tensor_scalar(erow_f[:, 2 * P:3 * P].bitcast(I32), erow_s[:, P:2 * P], 23, None,
                            ALU.logical_shift_left).then_inc(rows_cast, 1)
            after(d.tensor_scalar(tw3[:, :], tw[:, :], -1.0, None, ALU.mult))
            d.tensor_tensor(tw2[:, :], tw[:, :], tw3[:, :], ALU.min).then_inc(tw_dve, 1)
            v.wait_ge(tw_act, 1)
            d.tensor_scalar(tw2[:, :], tw2[:, :], 1.0, None, ALU.add).then_inc(tw_dve, 1)
            v.wait_ge(tw_act, 2)
            v.wait_ge(tw_dve, 2)
            after(d.tensor_scalar(tw3[:, :], tw[:, :], 0.0, None, ALU.max))
            after(d.tensor_tensor(tw3[:, :], tw3[:, :], tw2[:, :], ALU.add))
            after(d.tensor_scalar(tw[:, :], tw3[:, :], 1.0 / SCORE_SCALE, None, ALU.mult))
            v.wait_ge(cols_turned, 4)
            after(d.tensor_copy(cols[:, :], bank[7][:, 0:4 * EC]))
            after(d.scalar_tensor_tensor(key_col[:, :], cols[:, C_SRC:C_SRC + EC], float(N),
                                         cols[:, C_DST:C_DST + EC], ALU.mult, ALU.add))
            after(d.tensor_scalar(w_digit[:, :], cols[:, C_REL:C_REL + EC], float(DIGIT_BITS * 2 ** 23),
                                  float(127 * 2 ** 23), ALU.mult, ALU.add))
            power8 = w_digit[:, :].bitcast(F32)

            def take_tile(u, j):
                v.wait_ge(f_hi, u + 1)
                d.scalar_tensor_tensor(t1_lo[:, bass.ds(u * N, N)], bank[j % RING][:, 0:N],
                                       bias_col[:, bass.ds(u, 1)], t1_hi[:, bass.ds(u * N, N)],
                                       ALU.add, ALU.subtract).then_inc(f_lo, 1)

            for u in range(KT):
                take_tile(u, u)
            v.wait_ge(keys_loaded, 8 * 16)
            after(d.scalar_tensor_tensor(key_row[:, :], key_src[:, :], float(N), key_dst[:, :],
                                         ALU.mult, ALU.add))

            def find_later(c):
                d.scalar_tensor_tensor(dup_junk[:, :], key_row[:, bass.ds(c * P, P)],
                                       key_col[:, bass.ds(c, 1)], later[:, :],
                                       ALU.is_equal, ALU.mult, accum_out=dup[:, bass.ds(c, 1)])\
                 .then_inc(dve, 1)

            def one_hots(c, n, slot, w, w_at):
                v.wait_ge(oh_used, n + 1)
                s = slice(slot * N, (slot + 1) * N)
                d.tensor_scalar(src_oh[:, s], iota16[:, :], cols[:, bass.ds(c + C_SRC, 1)], None,
                                ALU.is_equal).then_inc(oh_ready, 1)
                d.tensor_scalar(dst_oh[:, s], iota16[:, :], cols[:, bass.ds(c + C_DST, 1)],
                                w[:, bass.ds(c + w_at, 1)], ALU.is_equal, ALU.mult).then_inc(oh_ready, 1)

            chained0 = chained[0]
            with v.Fori(1, 3) as i:
                for j in range(KT):
                    c0 = i * (OH * KT) + (j - KT) * OH
                    for c in range(OH):
                        one_hots(c0 + c, c0 + c, c, power8, 0)
                    take_tile(i * KT + j, j)
                    for c in range(OH):
                        v.wait_ge(dve, c0 + (c + chained0))
                        find_later(c0 + c)
            chained[0] += 2 * OH * KT
            for c in range(2 * OH * KT, EC):
                one_hots(c, c, c % OH, power8, 0)
                v.wait_ge(dve, chained[0])
                find_later(c)
                chained[0] += 1
            v.wait_ge(dve, chained[0])
            after(d.scalar_tensor_tensor(w_code[:, :], dup[:, :], 0.0, cols[:, C_CODE:C_CODE + EC],
                                         ALU.is_equal, ALU.mult))

            def take_tile2(u, j):
                v.wait_ge(f_hi, u + (U_F2 + 1))
                d.scalar_tensor_tensor(t2_lo[:, bass.ds(u * N, N)], bank[j % RING][:, 0:N],
                                       bias_col[:, bass.ds(u + U_F2, 1)],
                                       t2_hi[:, bass.ds(u * N, N)],
                                       ALU.add, ALU.subtract).then_inc(f_lo, 1)

            for j in range(KT):
                if j == 2:
                    v.wait_ge(oh_used, OH + EC)
                    for t in range(NT):
                        d.tensor_scalar(digits_raw[:, t * N:(t + 1) * N], bank[4 + t][:, 0:N], DIGIT_LIMIT, None,
                                        ALU.min).then_inc(digits_saved, 1)
                if j >= MASK_TILE:
                    for c in range(OH):
                        n = (j - MASK_TILE) * OH + c
                        one_hots(n, EC + n, c, w_code, 0)
                take_tile2(j, j)
            with v.Fori(0, KT // RING) as i:
                for j in range(RING):
                    for c in range(OH):
                        n = i * (RING * OH) + ((KT - MASK_TILE + j) * OH + c)
                        one_hots(n, n + EC, c, w_code, 0)
                    take_tile2(i * RING + (KT + j), j)
            v.wait_ge(unit_done, U_F2 + KT)
            v.wait_ge(digits_saved, NT)
            after(d.tensor_copy(digits[:, :], digits_raw[:, :]))
            for n in range((2 * KT - MASK_TILE) * OH, EC):
                one_hots(n, EC + n, n % OH, w_code, 0)

            v.wait_ge(oh_used, OH + 2 * EC)
            for t in range(NT):
                s = slice(t * N, (t + 1) * N)
                d.tensor_scalar(m_code[:, s], bank[4 + t][:, 0:N].bitcast(I32), 23, None,
                                ALU.logical_shift_right).then_inc(mask_read, 1)
            v.wait_ge(mask_read, NT)
            for t in range(NT):
                q = m_code[:, t * N + t * P:t * N + (t + 1) * P]
                after(d.scalar_tensor_tensor(q, ident[:, :], 3.0, q, ALU.mult, ALU.max))
            after(d.tensor_scalar(m_kind[:, :], m_code[:, :], 3, None, ALU.bitwise_and))
            after(d.tensor_scalar(mask[:, :], m_code[:, :], 0.0, ABSENT, ALU.is_equal, ALU.mult))
            for kind in range(4):
                after(d.tensor_scalar(m_part[:, :], m_kind[:, :], float(kind), tw[:, kind:kind + 1],
                                      ALU.is_equal, ALU.mult))
                ins = d.tensor_tensor(mask[:, :], mask[:, :], m_part[:, :], ALU.add)
                if kind < 3:
                    after(ins)
                else:
                    ins.then_inc(mask_made, 1)
            v.wait_ge(mask_made, 1)
            for n in range(2 * NT):
                s = slice(n * HALF, (n + 1) * HALF)
                v.wait_ge(v_hi, n + 1)
                d.tensor_tensor(v2_lo[:, s], bank[4 + n % 4][:, :], v2_hi[:, s],
                                ALU.subtract).then_inc(v_ready, 1)

            def logits(h):
                b = h % 3
                if h >= 2:
                    v.wait_ge(exp_done, NT * (h - 1))
                for t in range(NT):
                    m = h * NT + t
                    v.wait_ge(score_done, m + 1)
                    d.tensor_tensor_reduce(logit[:, (h % 2 * NT + t) * N:(h % 2 * NT + t + 1) * N],
                                           bank[m % 4][:, 0:N], mask[:, t * N:(t + 1) * N],
                                           1.0, ABSENT * 10, ALU.add, ALU.max,
                                           sm[:, 12 * b + t:12 * b + t + 1]).then_inc(logit_made, 1)
                v.wait_ge(logit_made, NT * (h + 1))
                d.tensor_scalar(sm[:, 12 * b + 3:12 * b + 6], sm[:, 12 * b:12 * b + 3], -SCORE_SCALE, None,
                                ALU.mult).then_inc(negmax, 1)

            def sums(h):
                b = h % 3
                v.wait_ge(exp_done, NT * (h + 1))
                d.reciprocal(sm[:, 12 * b + 9:12 * b + 12], sm[:, 12 * b + 6:12 * b + 9]).then_inc(rsum, 1)

            def take_pt_lo(h):
                b = h % 2
                for m in range(NT):
                    v.wait_ge(pt_hi_made, NT * h + m + 1)
                    s = slice((b * NT + m) * N, (b * NT + m + 1) * N)
                    d.tensor_tensor(pt_lo[:, s], bank[4 + m][:, 0:N], pt_hi[:, s],
                                    ALU.subtract).then_inc(pt_ready, 1)

            def take_o_lo(h):
                v.wait_ge(o_hi_made, h + 1)
                q = slice(DH * (h % 2), DH * (h % 2) + DH)
                s = slice(h // 2 * N, (h // 2 + 1) * N)
                d.tensor_tensor(o_lo[q, s], bank[7][q, 0:N], o_hi[q, s], ALU.subtract).then_inc(o_ready, 1)

            for i in range(H + 4):
                if i < H:
                    logits(i)
                if 1 <= i <= H:
                    sums(i - 1)
                if 3 <= i < H + 3:
                    take_pt_lo(i - 3)
                if i >= 4:
                    take_o_lo(i - 4)
                if i >= H:
                    for m in range((i - H) * DIGIT_STEPS, (i - H + 1) * DIGIT_STEPS):
                        if m >= NT:
                            v.wait_ge(digit_taken, m - NT + 1)
                        s = slice(m % NT * N, (m % NT + 1) * N)
                        d.tensor_scalar(one_digit[:, s], digits[:, s], DIGIT_BITS * (m // NT), 2 ** DIGIT_BITS - 1,
                                        ALU.logical_shift_right, ALU.bitwise_and).then_inc(digit_cut, 1)

            v.wait_ge(xres_loaded, 16)
            v.wait_ge(bo_loaded, 16)
            for t in range(NT):
                ins = d.tensor_tensor(x1[:, t * D:(t + 1) * D], x1[:, t * D:(t + 1) * D], row_bias[:, :],
                                      ALU.add)
                after(ins)
            d.tensor_copy(dup_junk[:, 0:1], sm[:, 0:1]).then_inc(xb_made, 1)

            def norm_stats(n, t, src):
                for half in range(2):
                    ins = d.bn_stats(stats[:, 12 * t + 6 * half:12 * t + 6 * half + 6],
                                     src[:, t * D + half * HALF:t * D + (half + 1) * HALF])
                    after(ins)
                after(d.bn_aggr(mv[:, 2 * t:2 * t + 2], stats[:, 12 * t:12 * t + 12]))
                d.tensor_scalar(vare[:, t:t + 1], mv[:, 2 * t + 1:2 * t + 2], EPS, None,
                                ALU.add).then_inc(var_made, 1)

            v.wait_ge(total_made, 1)
            after(d.tensor_reduce(digit_total[:, :], bank[7][:, 0:R * NT], AX.X, ALU.add))
            d.tensor_scalar(counted[:, :], digit_total[:, :], float(E), None,
                            ALU.is_equal).then_inc(counted_made, 1)
            v.wait_ge(unit_done, U_ROOT)
            for t in range(NT):
                for half in range(2):
                    s = slice(t * D + half * HALF, t * D + (half + 1) * HALF)
                    ins = d.tensor_tensor(x1[:, s], bank[2 * t + half][:, :], x1[:, s], ALU.add)
                    ins.then_inc(res_made, 1)
                v.wait_ge(res_made, 2 * (t + 1))
                norm_stats(0, t, x1)
            for t in range(NT):
                v.wait_ge(rstd_made, t + 1)
                s = slice(t * D, (t + 1) * D)
                d.tensor_scalar(x1[:, s], x1[:, s], mv[:, 2 * t:2 * t + 1], rstd[:, t:t + 1],
                                ALU.subtract, ALU.mult).then_inc(x1_made, 1)
            for k in range(KT):
                v.wait_ge(x1t_hi_made, k + 1)
                s = slice(k * N, (k + 1) * N)
                d.tensor_tensor(x1t_lo[:, s], bank[6 + k % 2][:, 0:N], x1t_hi[:, s],
                                ALU.subtract).then_inc(x1t_ready, 1)

            def general_counts():
                waited = [0]

                def then(ins):
                    waited[0] += 1
                    ins.then_inc(general, 1)
                    v.wait_ge(general, waited[0])

                for p in range(R // 2):
                    weight = w_rel[:, p * EC:(p + 1) * EC]
                    rel = cols[:, C_REL:C_REL + EC]
                    then(d.tensor_scalar(weight, rel, float(2 * p + 1), float(FIELD), ALU.is_equal, ALU.mult))
                    then(d.scalar_tensor_tensor(weight, rel, float(2 * p), weight, ALU.is_equal, ALU.add))

                def decode(n):
                    half, p = divmod(n, 4)
                    for t in range(NT):
                        m = n * NT + t
                        v.wait_ge(hist_cast, m + 1)
                        both = both_i[:, (m % 2) * N:(m % 2 + 1) * N]
                        then(d.tensor_scalar(low_i[:, :], both, FIELD - 1, None, ALU.bitwise_and))
                        d.tensor_scalar(high_i[:, :], both, FIELD_BITS, None, ALU.logical_shift_right)\
                         .then_inc(hist_decoded, 1)
                        v.wait_ge(hist_decoded, m + 1)
                        for r, part in ((2 * p, low_i), (2 * p + 1, high_i)):
                            q = a_cnt[:, (r * NT + t) * N:(r * NT + t + 1) * N]
                            if half == 0:
                                ins = d.tensor_copy(q, part[:, :])
                            else:
                                ins = d.tensor_tensor(q, q, part[:, :], ALU.add)
                            then(ins)

                used = 2 * EC
                for n in range(8):
                    half, p = divmod(n, 4)
                    c0, c1 = HALVES[half]
                    with v.Fori(0, (c1 - c0) // OH) as i:
                        for j in range(OH):
                            one_hots(i * OH + (c0 + j), i * OH + (used + j), j, w_rel, p * EC)
                    used += c1 - c0
                    if n >= 1:
                        decode(n - 1)
                decode(7)

            v.wait_ge(counted_made, 1)
            stands = v.value_load(counted[0:1, 0:1], min_val=0, max_val=1)
            with v.If(stands == 0):
                general_counts()
            d.memset(dup_junk[:, 0:1], 0.0).then_inc(cnt_made, 1)

            def normalise(r):
                rc = rcount[:, (r % 2) * N:(r % 2 + 1) * N]
                v.wait_ge(cnt_summed, r + 1)
                after(d.tensor_scalar(rc, bank[6 + r % 2][:, 0:N], 1.0, None, ALU.max))
                after(d.reciprocal(rc, rc))
                for t in range(NT):
                    q = a_cnt[:, (r * NT + t) * N:(r * NT + t + 1) * N]
                    ins = d.tensor_tensor(q, q, rc, ALU.mult)
                    if t < NT - 1:
                        after(ins)
                    else:
                        ins.then_inc(a_norm, 1)

            def split_a(r):
                s = slice(r * NT * N, (r + 1) * NT * N)
                v.wait_ge(a_hi_made, r + 1)
                d.tensor_tensor(a_lo[:, s], a_cnt[:, s], a_hi[:, s], ALU.subtract).then_inc(a_ready, 1)

            for r in range(R):
                normalise(r)
                if r >= 1:
                    split_a(r - 1)
            split_a(R - 1)
            v.wait_ge(x1h_hi_made, 1)
            d.tensor_tensor(x1h_lo[:, :], x1[:, :], x1h_hi[:, :], ALU.subtract).then_inc(x1h_ready, 1)

            with v.Fori(0, R) as r:
                for k in range(KT):
                    v.wait_ge(mean_hi_made, r * KT + (k + 1))
                    b = k % 2
                    d.tensor_tensor(mean_lo[:, b * N:(b + 1) * N], bank[6 + b][:, 0:N],
                                    mean_hi[:, b * N:(b + 1) * N], ALU.subtract).then_inc(mean_ready, 1)
            v.wait_ge(rb_loaded, 16)
            v.wait_ge(unit_done, U_GX)
            for n in range(2 * NT):
                s = slice(n * HALF, (n + 1) * HALF)
                d.tensor_tensor(u_nat[:, s], bank[n][:, :], row_bias[:, (n % 2) * HALF:(n % 2 + 1) * HALF],
                                ALU.add).then_inc(u_made, 1)
            for k in range(KT):
                v.wait_ge(ut_hi_made, k + 1)
                s = slice(k * N, (k + 1) * N)
                d.tensor_tensor(ut_lo[:, s], bank[6 + k % 2][:, 0:N], ut_hi[:, s],
                                ALU.subtract).then_inc(ut_ready, 1)
            v.wait_ge(bg_loaded, 16)
            for t in range(NT):
                s = slice(t * D, (t + 1) * D)
                v.wait_ge(tanh_made, t + 1)
                after(d.tensor_tensor(gated[:, s], gated[:, s], x1[:, s], ALU.subtract))
                after(d.tensor_tensor(fixed[:, s], gated[:, s], row_bias[:, :], ALU.mult))
                after(d.scalar_tensor_tensor(fixed[:, s], x1[:, s], 2.0, fixed[:, s], ALU.mult, ALU.add))
            for t in range(NT):
                v.wait_ge(z_summed, t + 1)
                for half in range(2):
                    s = slice(t * D + half * HALF, t * D + (half + 1) * HALF)
                    after(d.tensor_tensor(result[:, s], bank[2 * t + half][:, :], gated[:, s], ALU.mult))
                s = slice(t * D, (t + 1) * D)
                after(d.tensor_tensor(result[:, s], result[:, s], fixed[:, s], ALU.add))
                norm_stats(NT, t, result)
                v.wait_ge(rstd_made, NT + t + 1)
                d.tensor_scalar(result[:, s], result[:, s], mv[:, 2 * t:2 * t + 1], rstd[:, t:t + 1],
                                ALU.subtract, ALU.mult).then_inc(out_made, 1)

        @block.tensor
        def _(pe):
            mm = nc.tensor.matmul

            def three(dst, l_hi, l_lo, r_hi, r_lo, start, stop):
                mm(dst, l_hi, r_hi, start=start, stop=False)
                mm(dst, l_hi, r_lo, start=False, stop=False)
                return mm(dst, l_lo, r_hi, start=False, stop=stop)

            def f_unit(u, j, src_hi, src_lo, at, piecewise=False):
                pe.wait_ge(lo_split, u + 1)
                for k in range(KT):
                    if piecewise and k % (KT // XC) == 0:
                        pe.wait_ge(x_ready, k // (KT // XC) + 1)
                    w = slice((j % RING) * UNIT + k * P, (j % RING) * UNIT + (k + 1) * P)
                    m = bass.ds(at + k * N, N)
                    last = three(bank[j % RING][:, 0:N], w_hi[:, w], w_lo[:, w], src_hi[:, m], src_lo[:, m],
                                 k == 0, k == KT - 1)
                last.then_inc(unit_done, 1)

            pe.wait_ge(f_lo, 1)
            f_unit(0, 0, xt_hi, xt_lo, 0, piecewise=True)
            pe.wait_ge(rows_cast, 4)
            pe.wait_ge(const_made, 7)
            for n in range(4):
                nc.tensor.transpose(bank[7][:, n * EC:(n + 1) * EC], erow_f[:, n * P:(n + 1) * P],
                                    ident[0:EC, 0:EC]).then_inc(cols_turned, 1)
            for j in range(1, KT):
                pe.wait_ge(f_lo, j + 1)
                f_unit(j, j, xt_hi, xt_lo, 0)
            def chunk(n, slot, start, stop, first=4):
                pe.wait_ge(oh_ready, (n + 1) * 2)
                m = slice(slot * N, (slot + 1) * N)
                for t in range(NT):
                    last = mm(bank[first + t][:, 0:N], src_oh[:, slot * N + t * P:slot * N + (t + 1) * P],
                              dst_oh[:, m], start=start, stop=stop)
                last.then_inc(oh_used, 1)

            for j in range(RING):
                pe.wait_ge(f_lo, KT + j + 1)
                f_unit(KT + j, j, xt_hi, xt_lo, 0)
                for c in range(OH):
                    chunk(j * OH + c, c, j == 0 and c == 0, False)
            with pe.Fori(1, 2 * KT // RING) as i:
                for j in range(RING):
                    pe.wait_ge(f_lo, i * RING + (KT + j + 1))
                    f_unit(i * RING + (KT + j), j, xt_hi, xt_lo, 0)
                    for c in range(OH):
                        chunk(i * (RING * OH) + (j * OH + c), c, False, False)
            pe.wait_ge(f_lo, U_F2 + RING - KT)
            for j in range(KT):
                pe.wait_ge(f_lo, U_F2 + j + 1)
                f_unit(U_F2 + j, j, t1_hi, t1_lo, 0)
                if j == 0:
                    for n in range(2 * OH * KT, EC):
                        chunk(n, n % OH, False, n == EC - 1)
                if j >= MASK_TILE:
                    for c in range(OH):
                        n = (j - MASK_TILE) * OH + c
                        if n == 0:
                            pe.wait_ge(digits_saved, NT)
                        chunk(EC + n, c, n == 0, False)
            with pe.Fori(0, KT // RING) as i:
                for j in range(RING):
                    pe.wait_ge(f_lo, i * RING + (U_F2 + KT + j + 1))
                    f_unit(i * RING + (U_F2 + KT + j), j, t1_hi, t1_lo, ACTS)
                    for c in range(OH):
                        n = i * (RING * OH) + ((KT - MASK_TILE + j) * OH + c)
                        chunk(n + EC, c, False, False)
            pe.wait_ge(f_lo, U_F2 + 2 * KT + RING)
            mask_left = list(range((2 * KT - MASK_TILE) * OH, EC))
            for j in range(KT):
                if j >= RING:
                    pe.wait_ge(v_ev, j - RING + 1)
                f_unit(U_F2 + 2 * KT + j, j, t1_hi, t1_lo, 2 * ACTS)
                for n in mask_left[j * OH:(j + 1) * OH]:
                    chunk(EC + n, n % OH, False, n == EC - 1)
            pe.wait_ge(v_ev, KT)
            pe.wait_ge(mask_read, NT)
            for n in range(2 * NT):
                t, half = divmod(n, 2)
                if n >= 4:
                    pe.wait_ge(v_ready, n - 3)
                for q in range(4):
                    o = half * 4 + q
                    last = nc.tensor.transpose(bank[4 + n % 4][:, q * P:(q + 1) * P],
                                               v2t[:, o * N + t * P:o * N + (t + 1) * P], ident[:, :])
                last.then_inc(v_turned, 1)
            pe.wait_ge(v_ready, 2 * NT)

            def scores(h):
                q = slice(DH * (h % 2), DH * (h % 2) + DH)
                for t in range(NT):
                    m = h * NT + t
                    if m >= 4:
                        pe.wait_ge(logit_made, m - 3)
                    n0 = h // 2 * N
                    sq = slice(n0 + t * P, n0 + (t + 1) * P)
                    sk = slice(ACTS + n0, ACTS + n0 + N)
                    three(bank[m % 4][:, 0:N], t2_hi[q, sq], t2_lo[q, sq], t2_hi[q, sk], t2_lo[q, sk],
                          True, True).then_inc(score_done, 1)

            def turn_p(h):
                b = h % 3
                for m in range(NT):
                    if h >= 1:
                        pe.wait_ge(pt_ready, NT * (h - 1) + m + 1)
                    for t in range(NT):
                        pe.wait_ge(prob_ready, NT * h + t + 1)
                        s0 = t * N + m * P
                        last = nc.tensor.transpose(bank[4 + m][:, t * P:(t + 1) * P],
                                                   prob[b][:, s0:s0 + P], ident[:, :])
                    last.then_inc(p_turned, 1)

            def weigh_v(h):
                b = h % 2
                if h >= 1:
                    pe.wait_ge(o_ready, h)
                for m in range(NT):
                    pe.wait_ge(pt_ready, NT * h + m + 1)
                    sv = slice(m * D + h // 2 * P, m * D + (h // 2 + 1) * P)
                    s = slice((b * NT + m) * N, (b * NT + m + 1) * N)
                    last = three(bank[7][:, 0:N], v2_hi[:, sv], v2_lo[:, sv], pt_hi[:, s], pt_lo[:, s],
                                 m == 0, m == NT - 1)
                last.then_inc(pv_done, 1)

            for i in range(H + 4):
                if i < H:
                    scores(i)
                if 3 <= i < H + 3:
                    turn_p(i - 3)
                if i >= 4:
                    weigh_v(i - 4)

            def n_unit(u, l_hi, l_lo, at, step, start, stop, wait_bank=None):
                pe.wait_ge(lo_split, u + 1)
                w0 = (u % RING) * UNIT if isinstance(u, int) else None
                return n_body(w0, l_hi, l_lo, at, start, stop, wait_bank)

            def n_body(w0, l_hi, l_lo, at, start, stop, wait_bank=None, each=None):
                for t in range(NT):
                    if wait_bank:
                        wait_bank(t)
                    s = slice(at + t * P, at + (t + 1) * P)
                    for half in range(2):
                        w = slice(w0 + half * HALF, w0 + (half + 1) * HALF)
                        last = three(bank[2 * t + half][:, :], l_hi[:, s], l_lo[:, s], w_hi[:, w],
                                     w_lo[:, w], start, stop)
                    if each is not None and t < NT - 1:
                        last.then_inc(each, 1)
                return last

            pe.wait_ge(o_ready, H)
            pe.wait_ge(logit_made, NT * H)
            pe.wait_ge(pt_ready, NT * H)
            for k in range(KT):
                n_unit(U_WO + k, o_hi, o_lo, k * N, 0, k == 0, k == KT - 1).then_inc(unit_done, 1)
            pe.wait_ge(digit_taken, R * NT)
            mm(bank[7][:, 0:R * NT], ones[:, :], digit_sum[:, :], start=True, stop=True).then_inc(total_made, 1)
            pe.wait_ge(x1_made, NT)
            for k in range(KT):
                if k >= 2:
                    pe.wait_ge(x1t_ready, k - 1)
                for t in range(NT):
                    last = nc.tensor.transpose(bank[6 + k % 2][:, t * P:(t + 1) * P],
                                               x1[:, t * D + k * P:t * D + (k + 1) * P], ident[:, :])
                last.then_inc(x1_turned, 1)
            pe.wait_ge(counted_made, 1)
            stands = pe.value_load(counted[0:1, 0:1], min_val=0, max_val=1)
            with pe.If(stands == 0):
                used = 2 * EC
                for n in range(8):
                    c0, c1 = HALVES[n // 4]
                    first = (n % 2) * NT
                    if n >= 2:
                        pe.wait_ge(hist_cast, NT * (n - 1))
                    for j in range(OH):
                        chunk(used + j, j, j == 0, False, first)
                    with pe.Fori(1, (c1 - c0) // OH - 1) as i:
                        for j in range(OH):
                            chunk(i * OH + (used + j), j, False, False, first)
                    for j in range(OH):
                        chunk(used + c1 - c0 - OH + j, j, False, j == OH - 1, first)
                    used += c1 - c0
            pe.wait_ge(cnt_made, 1)

            def count(r):
                if r >= 2:
                    pe.wait_ge(a_norm, r - 1)
                for t in range(NT):
                    last = mm(bank[6 + r % 2][:, 0:N], ones[:, :],
                              a_cnt[:, (r * NT + t) * N:(r * NT + t + 1) * N], start=t == 0, stop=t == NT - 1)
                last.then_inc(cnt_summed, 1)

            pe.wait_ge(x1t_ready, KT)
            count(0)
            count(1)
            for k in range(KT):
                n_unit(U_ROOT + k, x1t_hi, x1t_lo, k * N, 0, k == 0, False).then_inc(unit_done, 1)
                if k + 2 < R:
                    count(k + 2)
            pe.wait_ge(x1h_ready, 1)

            def aggregate(n, k, at):
                pe.wait_ge(mean_ready, n)
                for s_ in range(NT):
                    s = slice(s_ * D + k * P, s_ * D + (k + 1) * P)
                    m = bass.ds(at + s_ * N, N)
                    last = three(bank[6 + k % 2][:, 0:N], x1h_hi[:, s], x1h_lo[:, s], a_hi[:, m], a_lo[:, m],
                                 s_ == 0, s_ == NT - 1)
                last.then_inc(agg_done, 1)

            def weigh_mean(n, k, stop):
                pe.wait_ge(mean_ready, n + 2)
                pe.wait_ge(lo_split, n + (U_REL + 1))
                n_body((k % RING) * UNIT, mean_hi, mean_lo, (k % 2) * N, False, stop).then_inc(unit_done, 1)

            def first_aggregate():
                for s_ in range(NT):
                    last = three(bank[6][:, 0:N], x1h_hi[:, s_ * D:s_ * D + P], x1h_lo[:, s_ * D:s_ * D + P],
                                 a_hi[:, s_ * N:(s_ + 1) * N], a_lo[:, s_ * N:(s_ + 1) * N],
                                 s_ == 0, s_ == NT - 1)
                last.then_inc(agg_done, 1)

            first_aggregate()
            with pe.Fori(0, R - 1) as r:
                for k in range(KT):
                    n = r * KT + k
                    aggregate(n + 1, (k + 1) % KT, (r + (1 if k == KT - 1 else 0)) * (NT * N))
                    weigh_mean(n, k, False)
            for k in range(KT):
                n = (R - 1) * KT + k
                if k < KT - 1:
                    aggregate(n + 1, k + 1, (R - 1) * NT * N)
                weigh_mean(n, k, k == KT - 1)

            for k in range(KT):
                n_unit(U_GX + k, x1t_hi, x1t_lo, k * N, 0, k == 0, False,
                       (lambda t: pe.wait_ge(u_made, 2 * t + 2)) if k == 0 else None).then_inc(unit_done, 1)
                if k == 0:
                    for kk in range(KT):
                        if kk >= 2:
                            pe.wait_ge(ut_ready, kk - 1)
                        for t in range(NT):
                            last = nc.tensor.transpose(
                                bank[6 + kk % 2][:, t * P:(t + 1) * P],
                                u_nat[:, t * D + kk * P:t * D + (kk + 1) * P], ident[:, :])
                        last.then_inc(u_turned, 1)
            pe.wait_ge(ut_ready, KT)
            for k in range(KT):
                pe.wait_ge(lo_split, U_GU + k + 1)
                last = n_body((k % RING) * UNIT, ut_hi, ut_lo, k * N, False, k == KT - 1, None,
                              z_summed if k == KT - 1 else None)
                last.then_inc(unit_done if k < KT - 1 else z_summed, 1)


def kernel(**inputs):
    import numpy as np
    import concourse.bacc as bacc
    from concourse.bass_utils import run_bass_kernel_spmd as run

    i = {k: np.asarray(v) for k, v in inputs.items()}
    p, n, d = 128, 384, 1024
    kt, nt = d // p, n // p
    e = i["src"].shape[0]

    def f_order(w):
        return w.reshape(kt, p, kt, p).transpose(0, 3, 2, 1).reshape(kt, p, d)

    def n_order(w):
        return w.reshape(kt, p, d)

    g = {k[7:]: v for k, v in i.items() if k.startswith("L")}
    weights = np.concatenate(
        [f_order(g[k]) for k in ("wq", "wk", "wv", "wiq", "wik", "wiv")]
        + [n_order(g["wo"].T), n_order(g["root"])]
        + [n_order(w) for w in g["weight"]]
        + [n_order(g["w_gate"][d:]), n_order(g["w_gate"][:d])])
    arrays = {
        "x_nat": i["x"].reshape(nt, p, d).transpose(1, 0, 2).reshape(p, nt * d),
        "x_t": i["x"].T.reshape(kt, p, n).transpose(1, 0, 2).reshape(p, kt * n),
        "edges": np.concatenate([i[k].reshape(e // p, p) for k in ("src", "dst", "edge_type_5", "edge_type_8")], 1),
        "keys_src": i["src"], "keys_dst": i["dst"],
        "type_w": g["edge_type_weights"],
        "bias_f": np.concatenate([g[k].reshape(kt, p) for k in ("bq", "bk", "bv", "biq", "bik", "biv")]).T,
        "bo": g["bo"], "bias": g["bias"], "b_gate": g["b_gate"],
        "weights": weights,
    }
    arrays = {k: np.ascontiguousarray(v) for k, v in arrays.items()}
    nc = bacc.Bacc("TRN2", target_bir_lowering=False, num_devices=1)
    args = [nc.dram_tensor(k, v.shape, mybir.dt.from_np(v.dtype), kind="ExternalInput").ap()
            for k, v in arrays.items()]
    out = nc.dram_tensor("out_dram", (nt, p, d), mybir.dt.float32, kind="ExternalOutput").ap()
    build(nc, *args, out)
    r = run(nc, [arrays], core_ids=[0])
    return np.asarray(r.results[0]["out_dram"]).reshape(n, d)
```

```python
import concourse.bass as bass
from concourse import mybir
from contextlib import ExitStack

F32 = mybir.dt.float32
F32R = mybir.dt.float32r
BF16 = mybir.dt.bfloat16
F16 = mybir.dt.float16
I32 = mybir.dt.int32
ALU = mybir.AluOpType
ACT = mybir.ActivationFunctionType
AX = mybir.AxisListType

P = 128
N = 384
NT = N // P
D = 1024
KT = D // P
H = 16
DH = D // H
E = 6528
EC = E // P
R = 8
EPS = 1e-5
HALF = 512

UNIT = KT * P
RING = 4
U_F1 = 0
U_F2 = 3 * KT
U_V2 = 5 * KT
U_WO = 6 * KT
U_ROOT = 7 * KT
U_REL = 8 * KT
U_GX = U_REL + R * KT
U_GU = U_GX + KT
UNITS = U_GU + KT

XC = 4
WARM_UP = 20
KEY_PIECES = 4
OH = 3
DIGIT_BITS = 3
DIGIT_SLOTS = 4
DIGIT_LIMIT = float(2 ** (DIGIT_BITS * R))
HALVES = ((0, 27), (27, EC))
FIELD = 4096
FIELD_BITS = 12
ABSENT = -1e30
SCORE_SCALE = 1.0 / (DH ** 0.5)


def build(nc, x_nat, x_t, edges, keys_src, keys_dst, type_w, bias_f, bo, bias, b_gate, weights, out):
    ctx = ExitStack()
    with ctx:
        base = nc.sbuf_base
        base = (base + 31) // 32 * 32
        place = [base]

        def region(size):
            at = place[0]
            place[0] += (size + 31) // 32 * 32
            return at

        def sb(name, cols, dt, at=None, parts=P):
            size = cols * (2 if dt in (BF16, F16) else 4)
            if at is None:
                at = region(size)
            return nc.alloc_sbuf_tensor_at(name, [parts, cols], dt, offset=at)

        raw = sb("raw", RING * UNIT, F32)
        w_hi = sb("w_hi", RING * UNIT, F32R)
        w_lo = sb("w_lo", RING * UNIT, F32R)

        ACTS = KT * N
        z1 = region(2 * 3 * ACTS * 4)
        z1b = z1 + 3 * ACTS * 4
        z2 = region(4 * ACTS * 4)
        onehots = region(2 * OH * N * 2)
        z3 = region(2 * ACTS * 4)

        t1_hi = sb("t1_hi", 3 * ACTS, F32R, z1)
        t1_lo = sb("t1_lo", 3 * ACTS, F32R, z1b)
        erow_at = z1b + (3 * ACTS - 16 * P) * 4
        erow_i = sb("erow_i", 4 * P, I32, erow_at, EC)
        erow_f = sb("erow_f", 4 * P, F32, erow_at + 4 * P * 4, EC)
        erow_s = sb("erow_s", 3 * P, I32, erow_at + 8 * P * 4, EC)
        logit = sb("logit", 2 * NT * N, F32, z1)
        prob = [sb(f"prob{i}", NT * N, F32, at) for i, at in
                enumerate((z1 + 6 * NT * N * 4, z1 + 7 * NT * N * 4, z1b))]
        pt_hi = sb("pt_hi", 2 * NT * N, F32R, z1 + 2 * NT * N * 4)
        pt_lo = sb("pt_lo", 2 * NT * N, F32R, z1 + 4 * NT * N * 4)
        o_hi = sb("o_hi", ACTS, F32R, z1b + ACTS * 4)
        o_lo = sb("o_lo", ACTS, F32R, z1b + 2 * ACTS * 4)
        a_cnt = sb("a_cnt", R * NT * N, F32, z1)
        a_lo = sb("a_lo", R * NT * N, F32R, z1)
        x1h_hi = sb("x1h_hi", ACTS, F32R, z1b)
        x1h_lo = sb("x1h_lo", ACTS, F32R, z1b + ACTS * 4)
        rcount = sb("rcount", R * N, F32, z1b + 2 * ACTS * 4)
        u_nat = sb("u_nat", ACTS, F32, z1)
        gated = sb("gated", ACTS, F32, z1 + ACTS * 4)
        fixed = sb("fixed", ACTS, F32, z1 + 2 * ACTS * 4)
        digits = sb("digits", NT * N, I32, z1b + NT * N * 4)
        both_i = sb("both_i", 2 * N, I32, z1b)
        low_i = sb("low_i", N, I32, z1b + 2 * N * 4)
        high_i = sb("high_i", N, I32, z1b + 3 * N * 4)

        key_src = sb("key_src", E, I32, z2)
        key_row = sb("key_row", E, F32, z2)
        KEYS = E // KEY_PIECES
        key_dst = [sb(f"key_dst{c}", KEYS, I32, z2 + (E + c * KEYS) * 4 if c < KEY_PIECES - 1 else z1 + 2 * ACTS * 4)
                   for c in range(KEY_PIECES)]
        t2_hi = sb("t2_hi", 2 * ACTS, F32R, z2)
        t2_lo = sb("t2_lo", 2 * ACTS, F32R, z2 + 2 * ACTS * 4)
        a_hi = sb("a_hi", R * NT * N, F32R, z2)
        ut_hi = sb("ut_hi", ACTS, F32R, z2)
        ut_lo = sb("ut_lo", ACTS, F32R, z2 + ACTS * 4)
        result = sb("result", ACTS, F32, z2 + 2 * ACTS * 4)
        mean_hi = sb("mean_hi", 2 * N, F32R, z2 + 3 * ACTS * 4)
        mean_lo = sb("mean_lo", 2 * N, F32R, z2 + 3 * ACTS * 4 + 2 * N * 4)
        x1 = sb("x1", ACTS, F32, z2 + 3 * ACTS * 4)

        xt_hi = sb("xt_hi", ACTS, F32R, z3)
        xt_lo = sb("xt_lo", ACTS, F32R, z3 + ACTS * 4)
        v2_hi = sb("v2_hi", ACTS, F32R, z3)
        v2_lo = sb("v2_lo", ACTS, F32R, z3 + ACTS * 4)
        x1t_hi = sb("x1t_hi", ACTS, F32R, z3)
        x1t_lo = sb("x1t_lo", ACTS, F32R, z3 + ACTS * 4)
        one_digit = sb("one_digit", DIGIT_SLOTS * NT * N, I32, z3)

        src_oh = sb("src_oh", OH * N, BF16, onehots)
        dst_oh = sb("dst_oh", OH * N, BF16, onehots + OH * N * 2)

        mask_at = region(NT * N * 4)
        mask = sb("mask", NT * N, F32, mask_at)
        row_bias = sb("row_bias", D, F32, mask_at)
        digits_raw = sb("digits_raw", NT * N, I32, mask_at)
        m_code = sb("m_code", NT * N, I32, z1b + 2 * NT * N * 4)
        m_kind = sb("m_kind", NT * N, I32, z1b + 3 * NT * N * 4)
        m_part = sb("m_part", NT * N, F32, z1b + 4 * NT * N * 4)

        xt_raw = sb("xt_raw", ACTS, F32, z1)

        iota_i = sb("iota_i", N, I32, mask_at)
        iota16 = sb("iota16", N, F16)
        ident = sb("ident", P, F32)
        ones = sb("ones", P, F32)
        ones_r = sb("ones_r", P, F32R)
        later = sb("later", P, F32)
        cols = sb("cols", 4 * EC, F32)
        C_SRC, C_DST, C_CODE, C_REL = (i * EC for i in range(4))
        key_col = sb("key_col", EC, F32)
        dup = sb("dup", EC, F32)
        w_code = sb("w_code", EC, F32)
        w_digit = sb("w_digit", EC, I32)
        w_rel = sb("w_rel", 4 * EC, F32)
        digit_sum = sb("digit_sum", R, F32)
        digit_total = sb("digit_total", 1, F32)
        counted = sb("counted", 1, I32)
        dup_junk = sb("dup_junk", P, F32)
        bias_col = sb("bias_col", 6 * KT, F32)
        tw = sb("tw", 4, F32)
        tw2 = sb("tw2", 4, F32)
        tw3 = sb("tw3", 4, F32)
        sm = sb("sm", 3 * 4 * NT, F32)
        stats = sb("stats", NT * 12, F32)
        mv = sb("mv", NT * 2, F32)
        rstd = sb("rstd", NT, F32)
        nhalf = sb("nhalf", NT, F32)
        vare = sb("vare", NT, F32)
        negmean = sb("negmean", NT, F32)
        shift = sb("shift", NT, F32)
        assert place[0] <= nc.sbuf_usable_end, (place[0], nc.sbuf_usable_end)

        bank = [ctx.enter_context(nc.psum_tensor(f"bank{i}", [P, HALF], F32)) for i in range(8)]

        def sem(name):
            return ctx.enter_context(nc.semaphore(name))

        raw_loaded = [sem(f"raw_loaded{j}") for j in range(RING)]
        hi_split = sem("hi_split")
        lo_split = sem("lo_split")
        unit_done = sem("unit_done")
        x_loaded = [sem(f"x_loaded{c}") for c in range(XC)]
        small_loaded = sem("small_loaded")
        keys_loaded = [sem(f"keys_loaded{c}") for c in range(KEY_PIECES)]
        const_made = sem("const_made")
        warm_zeros = sem("warm_zeros")
        x_hi = sem("x_hi")
        x_ready = sem("x_ready")
        f_hi = sem("f_hi")
        f_lo = sem("f_lo")
        rows_cast = sem("rows_cast")
        cols_turned = sem("cols_turned")
        dup_found = sem("dup_found")
        dve = sem("dve")
        oh_ready = sem("oh_ready")
        oh_used = sem("oh_used")
        digits_saved = sem("digits_saved")
        mask_read = sem("mask_read")
        digit_cut = sem("digit_cut")
        digit_taken = sem("digit_taken")
        total_made = sem("total_made")
        counted_made = sem("counted_made")
        general = sem("general")
        hist_cast = sem("hist_cast")
        hist_decoded = sem("hist_decoded")
        mask_made = sem("mask_made")
        tw_act = sem("tw_act")
        tw_dve = sem("tw_dve")
        v_summed = sem("v_summed")
        v_hi = sem("v_hi")
        v_ready = sem("v_ready")
        score_done = sem("score_done")
        logit_made = sem("logit_made")
        negmax = sem("negmax")
        exp_done = sem("exp_done")
        rsum = sem("rsum")
        prob_ready = sem("prob_ready")
        p_turned = sem("p_turned")
        pt_hi_made = sem("pt_hi_made")
        pt_ready = sem("pt_ready")
        pv_done = sem("pv_done")
        o_hi_made = sem("o_hi_made")
        o_ready = sem("o_ready")
        xres_loaded = sem("xres_loaded")
        bo_loaded = sem("bo_loaded")
        rb_loaded = sem("rb_loaded")
        bg_loaded = sem("bg_loaded")
        xb_made = sem("xb_made")
        res_made = sem("res_made")
        var_made = sem("var_made")
        rstd_made = sem("rstd_made")
        shift_made = sem("shift_made")
        x1_made = sem("x1_made")
        x1_turned = sem("x1_turned")
        x1t_hi_made = sem("x1t_hi_made")
        x1t_ready = sem("x1t_ready")
        ones_made = sem("ones_made")
        wo_summed = sem("wo_summed")
        a_made = sem("a_made")
        a_hi_made = sem("a_hi_made")
        a_ready = sem("a_ready")
        cnt_summed = sem("cnt_summed")
        cnt_taken = sem("cnt_taken")
        rc_made = sem("rc_made")
        mean_scaled = sem("mean_scaled")
        x1h_hi_made = sem("x1h_hi_made")
        x1h_ready = sem("x1h_ready")
        agg_done = sem("agg_done")
        mean_hi_made = sem("mean_hi_made")
        mean_ready = sem("mean_ready")
        u_summed = sem("u_summed")
        u_made = sem("u_made")
        u_turned = sem("u_turned")
        ut_hi_made = sem("ut_hi_made")
        ut_ready = sem("ut_ready")
        tanh_made = sem("tanh_made")
        z_summed = sem("z_summed")
        out_made = sem("out_made")
        stored = sem("stored")

        CODE0 = 4

        def used_after(n):
            half, p = divmod(n, 4)
            return 2 * EC + 4 * sum(b - a for a, b in HALVES[:half]) + (p + 1) * (HALVES[half][1] - HALVES[half][0])

        FIRST_LO = 2
        MASK_GROUPS = (0, 0, 0, 2, 2, 2, 2, 0)
        MASK_BEFORE_K2 = sum(MASK_GROUPS)
        assert (MASK_BEFORE_K2 + KT + 1) * OH == EC
        CNT_BANKS = 4

        def turned(t, half):
            return bank[(4 if t == 2 else 6) + half][:, :].rearrange("p (k n) -> p k n", k=KT // 2)

        def x1t_tile(x1t, t, half):
            return x1t[:, half * (ACTS // 2):(half + 1) * (ACTS // 2)]\
                .rearrange("p (k n) -> p k n", k=KT // 2)[:, :, t * P:(t + 1) * P]

        block = ctx.enter_context(nc.Block())

        @block.sync
        def _(sp):
            for c in range(XC):
                s = slice(c * ACTS // XC, (c + 1) * ACTS // XC)
                sp.dma_start(xt_raw[:, s], x_t[:, s]).then_inc(x_loaded[c], 16)
                if c == 0:
                    sp.dma_start(raw[:, 0:UNIT], weights[0]).then_inc(raw_loaded[0], 16)
            for j in range(1, RING):
                sp.dma_start(raw[:, j * UNIT:(j + 1) * UNIT], weights[j]).then_inc(raw_loaded[j], 16)
            sp.dma_start(bias_col[:, :], bias_f).then_inc(small_loaded, 16)
            sp.dma_start(erow_i[:, :], edges).then_inc(small_loaded, 16)
            sp.dma_start(tw[:, :], type_w.partition_broadcast(P)).then_inc(small_loaded, 16)

            def load(u, j):
                sp.wait_ge(lo_split, u - RING + 1)
                sp.dma_start(raw[:, j * UNIT:(j + 1) * UNIT],
                             weights[bass.ds(u, 1)].rearrange("a p n -> (a p) n")).then_inc(raw_loaded[j], 16)

            for u in range(RING, RING + 2 * KEY_PIECES):
                load(u, u % RING)
                c, half = divmod(u - RING, 2)
                piece = slice(c * E // KEY_PIECES, (c + 1) * E // KEY_PIECES)
                if half == 0:
                    sp.dma_start(key_src[:, piece], keys_src[piece].partition_broadcast(P)).then_inc(keys_loaded[c], 16)
                else:
                    sp.dma_start(key_dst[c][:, :], keys_dst[piece].partition_broadcast(P)).then_inc(keys_loaded[c], 16)
            with sp.Fori(2 + 2 * KEY_PIECES // RING - 1, U_WO // RING + 1) as i:
                for j in range(RING):
                    load(i * RING + j, j)
            sp.wait_ge(score_done, H * NT)
            sp.dma_start(x1[:, :], x_nat).then_inc(xres_loaded, 16)
            sp.wait_ge(logit_made, H * NT)
            sp.dma_start(row_bias[:, :], bo.partition_broadcast(P)).then_inc(bo_loaded, 16)
            with sp.Fori(U_WO // RING + 1, U_REL // RING) as i:
                for j in range(RING):
                    load(i * RING + j, j)
            sp.wait_ge(xb_made, 1)
            sp.dma_start(row_bias[:, :], bias.partition_broadcast(P)).then_inc(rb_loaded, 16)
            with sp.Fori(U_REL // RING, U_GU // RING) as i:
                for j in range(RING):
                    load(i * RING + j, j)
            sp.wait_ge(u_made, 2 * NT)
            sp.dma_start(row_bias[:, :], b_gate.partition_broadcast(P)).then_inc(bg_loaded, 16)
            with sp.Fori(U_GU // RING, UNITS // RING) as i:
                for j in range(RING):
                    load(i * RING + j, j)
            for n in range(2 * NT):
                sp.wait_ge(out_made, n + 1)
                sp.dma_start(out[n // 2][:, n % 2 * HALF:(n % 2 + 1) * HALF],
                             result[:, n * HALF:(n + 1) * HALF]).then_inc(stored, 16)
            sp.wait_ge(stored, 16 * 2 * NT)

        @block.gpsimd
        def _(pool):
            g = nc.gpsimd
            g.memset(ident[:, :], 0.0).then_inc(const_made, 1)
            g.memset(ones[:, :], 1.0).then_inc(const_made, 1)
            g.memset(nhalf[:, :], -0.5).then_inc(const_made, 1)
            g.iota(iota_i[:, :], pattern=[[1, N]], base=0, channel_multiplier=0).then_inc(const_made, 1)
            g.iota(erow_s[:, 0:P], pattern=[[0, P]], base=CODE0, channel_multiplier=4).then_inc(const_made, 1)
            pool.wait_ge(const_made, 5)
            g.affine_select(out=ident[:, :], in_=ident[:, :], compare_op=ALU.not_equal, fill=1.0, base=0,
                            pattern=[[-1, P]], channel_multiplier=1).then_inc(const_made, 1)
            g.affine_select(out=later[:, :], in_=ones[:, :], compare_op=ALU.is_gt, fill=0.0, base=0,
                            pattern=[[1, P]], channel_multiplier=-1).then_inc(const_made, 1)

            def split_lo(u, j):
                pool.wait_ge(hi_split, u + 1)
                s = slice(j * UNIT, (j + 1) * UNIT)
                g.tensor_tensor(w_lo[:, s], raw[:, s], w_hi[:, s], ALU.subtract).then_inc(lo_split, 1)

            pool.wait_ge(lo_split, FIRST_LO)
            for j in range(FIRST_LO, RING):
                split_lo(j, j)
            with pool.Fori(1, U_WO // RING) as i:
                for j in range(RING):
                    split_lo(i * RING + j, j)
            for j in range(RING - 1):
                split_lo(U_WO + j, j)
            for h in range(H):
                b = h % 3
                pool.wait_ge(rsum, h + 1)
                for t in range(NT):
                    s = slice(t * N, (t + 1) * N)
                    r = sm[:, 12 * b + 9 + t:12 * b + 10 + t]
                    g.tensor_scalar(prob[b][:, s], prob[b][:, s], r, 1.0, ALU.mult, ALU.mult).then_inc(prob_ready, 1)
                if h == 2:
                    split_lo(U_WO + RING - 1, RING - 1)
            with pool.Fori(U_WO // RING + 1, U_ROOT // RING) as i:
                for j in range(RING):
                    split_lo(i * RING + j, j)
            for j in range(RING // 2):
                split_lo(U_ROOT + j, j)

            def inv_std(n):
                pool.wait_ge(var_made, n + 1)
                t = n % NT
                g.tensor_tensor(rstd[:, t:t + 1], vare[:, t:t + 1], nhalf[:, t:t + 1],
                                ALU.pow).then_inc(rstd_made, 1)
                pool.wait_ge(rstd_made, n + 1)
                g.tensor_tensor(shift[:, t:t + 1], negmean[:, t:t + 1], rstd[:, t:t + 1],
                                ALU.mult).then_inc(shift_made, 1)

            for t in range(NT):
                inv_std(t)
            for j in range(RING // 2, RING):
                split_lo(U_ROOT + j, j)
            with pool.Fori(U_ROOT // RING + 1, UNITS // RING - 1) as i:
                for j in range(RING):
                    split_lo(i * RING + j, j)
            for j in range(RING - 1):
                split_lo(UNITS - RING + j, j)
            for t in range(NT):
                inv_std(NT + t)

        @block.scalar
        def _(act):
            a = nc.scalar

            def split_hi(u, j, i):
                act.wait_ge(raw_loaded[j], 16 * (i + 1))
                s = slice(j * UNIT, (j + 1) * UNIT)
                a.activation(w_hi[:, s], raw[:, s], ACT.Copy).then_inc(hi_split, 1)

            def split_unit(u):
                if u < UNITS:
                    if u >= RING:
                        act.wait_ge(unit_done, u - RING + 1)
                    split_hi(u, u % RING, u // RING)

            for c in range(XC):
                s = slice(c * ACTS // XC, (c + 1) * ACTS // XC)
                act.wait_ge(x_loaded[c], 16)
                a.activation(xt_hi[:, s], xt_raw[:, s], ACT.Copy).then_inc(x_hi, 1)
                if c == 0:
                    split_unit(0)
            for u in range(1, RING):
                split_unit(u)
            act.wait_ge(tw_dve, 1)
            a.activation(tw2[:, :], tw2[:, :], ACT.Exp).then_inc(tw_act, 1)
            act.wait_ge(tw_dve, 2)
            a.activation(tw2[:, :], tw2[:, :], ACT.Ln).then_inc(tw_act, 1)

            def split_next(first_round, j, lead=0):
                act.wait_ge(raw_loaded[j % RING], (first_round + (j - lead) // RING + 2) * 16)
                s = slice(j % RING * UNIT, (j % RING + 1) * UNIT)
                a.activation(w_hi[:, s], raw[:, s], ACT.Copy).then_inc(hi_split, 1)

            with act.Fori(0, 3) as i:
                for j in range(KT):
                    u = i * KT + j
                    act.wait_ge(unit_done, u + 1)
                    a.activation(t1_hi[:, bass.ds(u * N, N)], bank[j % RING][:, 0:N], ACT.Identity,
                                 bias=bias_col[:, bass.ds(u, 1)]).then_inc(f_hi, 1)
                    split_next(i * 2, j)
            with act.Fori(0, 2) as i:
                for j in range(KT):
                    u = i * KT + j
                    act.wait_ge(unit_done, u + U_F2 + 1)
                    a.activation(t2_hi[:, bass.ds(u * N, N)], bank[j % RING][:, 0:N], ACT.Identity,
                                 bias=bias_col[:, bass.ds(u + U_F2, 1)]).then_inc(f_hi, 1)
                    split_next(i * 2 + U_F2 // RING, j)
            for u in range(U_V2 + RING, U_WO + RING - 2):
                split_unit(u)
            a.activation(tw2[:, :], tw2[:, :], ACT.Exp).then_inc(tw_act, 1)
            def take_v(n):
                a.activation(v2_hi[:, n * HALF:(n + 1) * HALF], bank[n][:, :], ACT.Copy).then_inc(v_hi, 1)

            for n in range(4):
                act.wait_ge(v_summed, n // 2 + 1)
                take_v(n)
            split_unit(U_WO + RING - 2)

            def softmax(h):
                b = h % 3
                act.wait_ge(negmax, h + 1)
                if h >= 3:
                    act.wait_ge(p_turned, NT * (h - 2))
                for t in range(NT):
                    s = slice((h % 2 * NT + t) * N, (h % 2 * NT + t + 1) * N)
                    a.activation(prob[b][:, t * N:(t + 1) * N], logit[:, s], ACT.Exp, scale=SCORE_SCALE,
                                 bias=sm[:, 12 * b + 3 + t:12 * b + 4 + t],
                                 accum_out=sm[:, 12 * b + 6 + t:12 * b + 7 + t]).then_inc(exp_done, 1)

            def take_pt(h):
                b = h % 2
                for m in range(NT):
                    act.wait_ge(p_turned, NT * h + m + 1)
                    if h >= 2 and m == 0:
                        act.wait_ge(pv_done, h - 1)
                    s = slice((b * NT + m) * N, (b * NT + m + 1) * N)
                    a.activation(pt_hi[:, s], bank[4 + m][:, 0:N], ACT.Copy).then_inc(pt_hi_made, 1)

            def take_o(h):
                act.wait_ge(pv_done, h + 1)
                q = slice(DH * (h % 2), DH * (h % 2) + DH)
                s = slice(h // 2 * N, (h // 2 + 1) * N)
                a.activation(o_hi[q, s], bank[7][q, 0:N], ACT.Identity,
                             bias=bias_col[q, 5 * KT + h // 2:5 * KT + h // 2 + 1]).then_inc(o_hi_made, 1)

            softmax(0)
            act.wait_ge(unit_done, U_WO)
            for n in range(4, 2 * NT):
                take_v(n)
            for i in range(2, H + 4):
                if i <= H:
                    softmax(i - 1)
                if i == 2:
                    split_unit(U_WO + RING - 1)
                if 3 <= i < H + 3:
                    take_pt(i - 3)
                if i >= 4:
                    take_o(i - 4)

            for r in range(R):
                if r < RING:
                    split_unit(U_WO + RING + r)
                act.wait_ge(digit_cut, r + 1)
                b = r % DIGIT_SLOTS
                a.activation(a_hi[:, r * NT * N:(r + 1) * NT * N], one_digit[:, b * NT * N:(b + 1) * NT * N],
                             ACT.Copy, accum_out=digit_sum[:, r:r + 1]).then_inc(digit_taken, 1)
            act.wait_ge(const_made, 7)
            a.activation(ones_r[:, :], ones[:, :], ACT.Copy).then_inc(ones_made, 1)
            split_unit(U_ROOT)
            split_unit(U_ROOT + 1)

            def apply_norm(n, s, src, done):
                act.wait_ge(shift_made, n + 1)
                t = n % NT
                a.activation(src[:, s], src[:, s], ACT.Identity, scale=rstd[:, t:t + 1],
                             bias=shift[:, t:t + 1]).then_inc(done, 1)

            apply_norm(0, slice(0, D), x1, x1_made)
            split_unit(U_ROOT + 2)

            def take_x1t(t):
                for half in range(2):
                    act.wait_ge(x1_turned, 2 * t + half + 1)
                    a.activation(x1t_tile(x1t_hi, t, half), turned(t, half), ACT.Copy).then_inc(x1t_hi_made, 1)

            take_x1t(0)
            apply_norm(1, slice(D, 2 * D), x1, x1_made)
            act.wait_ge(counted_made, 1)
            stands = act.value_load(counted[0:1, 0:1], min_val=0, max_val=1)
            with act.If(stands == 0):
                for n in range(2 * 4):
                    act.wait_ge(oh_used, OH + used_after(n))
                    for t in range(NT):
                        m = n * NT + t
                        if m >= 2:
                            act.wait_ge(hist_decoded, m - 1)
                        a.activation(both_i[:, (m % 2) * N:(m % 2 + 1) * N], bank[(n % 2) * NT + t][:, 0:N],
                                     ACT.Copy).then_inc(hist_cast, 1)
                act.wait_ge(a_made, 1)
                a.activation(a_hi[:, :], a_cnt[:, :], ACT.Copy).then_inc(a_hi_made, 1)
            for r in range(R):
                act.wait_ge(cnt_summed, r + 1)
                a.activation(rcount[:, r * N:(r + 1) * N], bank[2 + r % CNT_BANKS][:, 0:N],
                             ACT.Copy).then_inc(cnt_taken, 1)
            apply_norm(2, slice(2 * D, 3 * D), x1, x1_made)
            for t in range(1, NT):
                take_x1t(t)
            for u in range(U_ROOT + RING - 1, U_REL + RING - 1):
                split_unit(u)
                if u == U_ROOT + RING - 1:
                    a.activation(x1h_hi[:, :], x1[:, :], ACT.Copy).then_inc(x1h_hi_made, 1)

            def take_mean(n, k):
                act.wait_ge(mean_scaled, n + 1)
                act.wait_ge(unit_done, n + (U_REL - 1))
                b = k % 2
                a.activation(mean_hi[:, b * N:(b + 1) * N], bank[6 + b][:, 0:N],
                             ACT.Copy).then_inc(mean_hi_made, 1)

            with act.Fori(0, R) as r:
                for k in range(KT):
                    n = r * KT + k
                    take_mean(n, k)
                    act.wait_ge(unit_done, n + U_REL)
                    split_next(r * 2 + U_REL // RING, k + RING - 1, RING)
            act.wait_ge(unit_done, U_GX)
            split_unit(U_GX + RING - 1)
            for k in range(KT):
                act.wait_ge(u_turned, k + 1)
                a.activation(ut_hi[:, k * N:(k + 1) * N], bank[6 + k % 2][:, 0:N],
                             ACT.Copy).then_inc(ut_hi_made, 1)
                if k % 2:
                    split_unit(U_GX + RING + k // 2)
            for t in range(NT):
                s = slice(t * D, (t + 1) * D)
                a.activation(gated[:, s], u_nat[:, s], ACT.Tanh).then_inc(tanh_made, 1)
            for u in range(U_GX + 2 * RING, UNITS):
                split_unit(u)
            for n in range(2 * NT):
                apply_norm(NT + n // 2, slice(n * HALF, (n + 1) * HALF), result, out_made)

        @block.vector
        def _(v):
            d = nc.vector
            chained = [0]

            def after(ins):
                chained[0] += 1
                ins.then_inc(dve, 1)
                v.wait_ge(dve, chained[0])

            d.memset(src_oh[:, 0:N], 0.0).then_inc(warm_zeros, 1)
            d.memset(dup_junk[:, :], 0.0).then_inc(f_lo, RING)
            d.memset(sm[:, :], 0.0).then_inc(oh_used, OH)
            d.memset(rstd[:, :], 0.0).then_inc(mean_ready, 1)
            d.memset(dup[:, :], 0.0).then_inc(dup_found, 1)

            def first_lo(u):
                v.wait_ge(hi_split, u + 1)
                s = slice(u * UNIT, (u + 1) * UNIT)
                d.tensor_tensor(w_lo[:, s], raw[:, s], w_hi[:, s], ALU.subtract).then_inc(lo_split, 1)

            for c in range(XC):
                s = slice(c * ACTS // XC, (c + 1) * ACTS // XC)
                v.wait_ge(x_hi, c + 1)
                d.tensor_tensor(xt_lo[:, s], xt_raw[:, s], xt_hi[:, s], ALU.subtract).then_inc(x_ready, 1)
                if c == 0:
                    first_lo(0)
            for u in range(1, FIRST_LO):
                first_lo(u)

            v.wait_ge(small_loaded, 48)
            v.wait_ge(const_made, 5)
            d.tensor_copy(iota16[:, :], iota_i[:, :]).then_inc(rows_cast, 1)
            d.tensor_copy(erow_f[:, 0:2 * P], erow_i[:, 0:2 * P]).then_inc(rows_cast, 1)
            d.tensor_copy(erow_f[:, 3 * P:4 * P], erow_i[:, 3 * P:4 * P]).then_inc(rows_cast, 1)
            after(d.tensor_scalar(erow_s[:, P:2 * P], erow_i[:, 2 * P:3 * P], 3, None, ALU.add))
            after(d.tensor_scalar(erow_s[:, 2 * P:3 * P], erow_s[:, P:2 * P], 3, None, ALU.bitwise_and))
            after(d.tensor_tensor(erow_s[:, P:2 * P], erow_s[:, 2 * P:3 * P], erow_s[:, 0:P], ALU.add))
            d.tensor_scalar(erow_f[:, 2 * P:3 * P].bitcast(I32), erow_s[:, P:2 * P], 23, None,
                            ALU.logical_shift_left).then_inc(rows_cast, 1)
            after(d.tensor_scalar(tw3[:, :], tw[:, :], -1.0, None, ALU.mult))
            d.tensor_tensor(tw2[:, :], tw[:, :], tw3[:, :], ALU.min).then_inc(tw_dve, 1)
            v.wait_ge(tw_act, 1)
            d.tensor_scalar(tw2[:, :], tw2[:, :], 1.0, None, ALU.add).then_inc(tw_dve, 1)
            v.wait_ge(tw_act, 2)
            v.wait_ge(tw_dve, 2)
            after(d.tensor_scalar(tw3[:, :], tw[:, :], 0.0, None, ALU.max))
            after(d.tensor_tensor(tw3[:, :], tw3[:, :], tw2[:, :], ALU.add))
            after(d.tensor_scalar(tw[:, :], tw3[:, :], 1.0 / SCORE_SCALE, None, ALU.mult))
            v.wait_ge(cols_turned, 4)
            after(d.tensor_copy(cols[:, :], bank[7][:, 0:4 * EC]))
            after(d.scalar_tensor_tensor(key_col[:, :], cols[:, C_SRC:C_SRC + EC], float(N),
                                         cols[:, C_DST:C_DST + EC], ALU.mult, ALU.add))
            after(d.tensor_scalar(w_digit[:, :], cols[:, C_REL:C_REL + EC], float(DIGIT_BITS * 2 ** 23),
                                  float(127 * 2 ** 23), ALU.mult, ALU.add))
            power8 = w_digit[:, :].bitcast(F32)

            def take_tile(u, j):
                v.wait_ge(f_hi, u + 1)
                d.scalar_tensor_tensor(t1_lo[:, bass.ds(u * N, N)], bank[j % RING][:, 0:N],
                                       bias_col[:, bass.ds(u, 1)], t1_hi[:, bass.ds(u * N, N)],
                                       ALU.add, ALU.subtract).then_inc(f_lo, 1)

            def make_keys(c):
                v.wait_ge(keys_loaded[c], 2 * 16)
                s = slice(c * E // KEY_PIECES, (c + 1) * E // KEY_PIECES)
                after(d.scalar_tensor_tensor(key_row[:, s], key_src[:, s], float(N), key_dst[c][:, :],
                                             ALU.mult, ALU.add))

            for u in range(KT):
                take_tile(u, u)
            make_keys(0)

            def find_later(c):
                v.wait_ge(dup_found, c + 1)
                d.scalar_tensor_tensor(dup_junk[:, :], key_row[:, bass.ds(c * P, P)],
                                       key_col[:, bass.ds(c, 1)], later[:, :],
                                       ALU.is_equal, ALU.mult, accum_out=dup[:, bass.ds(c, 1)])\
                 .then_inc(dup_found, 1)

            def one_hots(c, n, slot, w, w_at):
                v.wait_ge(oh_used, n + 1)
                s = slice(slot * N, (slot + 1) * N)
                d.tensor_scalar(src_oh[:, s], iota16[:, :], cols[:, bass.ds(c + C_SRC, 1)], None,
                                ALU.is_equal).then_inc(oh_ready, 1)
                d.tensor_scalar(dst_oh[:, s], iota16[:, :], cols[:, bass.ds(c + C_DST, 1)],
                                w[:, bass.ds(c + w_at, 1)], ALU.is_equal, ALU.mult).then_inc(oh_ready, 1)

            def tile_and_chunks(u, c0, j):
                for c in range(OH):
                    one_hots(c0 + c, c0 + c, c, power8, 0)
                take_tile(u, j)
                for c in range(OH):
                    find_later(c0 + c)

            for j in range(KT):
                tile_and_chunks(KT + j, j * OH, j)
                if 1 <= j < KEY_PIECES:
                    make_keys(j)
            with v.Fori(0, KT // RING) as i:
                for j in range(RING):
                    tile_and_chunks(i * RING + (2 * KT + j), i * (RING * OH) + (KT + j) * OH, j)
            for c in range(2 * OH * KT, EC):
                one_hots(c, c, c % OH, power8, 0)
                find_later(c)
            v.wait_ge(dup_found, EC + 1)
            after(d.scalar_tensor_tensor(w_code[:, :], dup[:, :], 0.0, cols[:, C_CODE:C_CODE + EC],
                                         ALU.is_equal, ALU.mult))

            def take_tile2(u, j):
                v.wait_ge(f_hi, u + (U_F2 + 1))
                d.scalar_tensor_tensor(t2_lo[:, bass.ds(u * N, N)], bank[j % RING][:, 0:N],
                                       bias_col[:, bass.ds(u + U_F2, 1)],
                                       t2_hi[:, bass.ds(u * N, N)],
                                       ALU.add, ALU.subtract).then_inc(f_lo, 1)

            for j in range(KT):
                if j == 2:
                    v.wait_ge(oh_used, OH + EC)
                    for t in range(NT):
                        d.tensor_scalar(digits_raw[:, t * N:(t + 1) * N], bank[4 + t][:, 0:N], DIGIT_LIMIT, None,
                                        ALU.min).then_inc(digits_saved, 1)
                for n in range(sum(MASK_GROUPS[:j]) * OH, sum(MASK_GROUPS[:j + 1]) * OH):
                    one_hots(n, EC + n, n % OH, w_code, 0)
                take_tile2(j, j)
            with v.Fori(0, KT // RING) as i:
                for j in range(RING):
                    for c in range(OH):
                        n = i * (RING * OH) + ((MASK_BEFORE_K2 + j) * OH + c)
                        one_hots(n, n + EC, c, w_code, 0)
                    take_tile2(i * RING + (KT + j), j)
            for n in range(EC - OH, EC):
                one_hots(n, EC + n, n % OH, w_code, 0)

            v.wait_ge(oh_used, OH + 2 * EC)
            for t in range(NT):
                s = slice(t * N, (t + 1) * N)
                d.tensor_scalar(m_code[:, s], bank[4 + t][:, 0:N].bitcast(I32), 23, None,
                                ALU.logical_shift_right).then_inc(mask_read, 1)
            v.wait_ge(mask_read, NT)
            v.wait_ge(digits_saved, NT)
            after(d.tensor_copy(digits[:, :], digits_raw[:, :]))
            for t in range(NT):
                q = m_code[:, t * N + t * P:t * N + (t + 1) * P]
                after(d.scalar_tensor_tensor(q, ident[:, :], 3.0, q, ALU.mult, ALU.max))
            after(d.tensor_scalar(m_kind[:, :], m_code[:, :], 3, None, ALU.bitwise_and))
            after(d.tensor_scalar(mask[:, :], m_code[:, :], 0.0, ABSENT, ALU.is_equal, ALU.mult))
            for kind in range(4):
                after(d.tensor_scalar(m_part[:, :], m_kind[:, :], float(kind), tw[:, kind:kind + 1],
                                      ALU.is_equal, ALU.mult))
                ins = d.tensor_tensor(mask[:, :], mask[:, :], m_part[:, :], ALU.add)
                if kind < 3:
                    after(ins)
                else:
                    ins.then_inc(mask_made, 1)
            v.wait_ge(mask_made, 1)
            def take_v_lo(n):
                s = slice(n * HALF, (n + 1) * HALF)
                v.wait_ge(v_hi, n + 1)
                d.tensor_tensor(v2_lo[:, s], bank[n][:, :], v2_hi[:, s],
                                ALU.subtract).then_inc(v_ready, 1)

            def logits(h):
                b = h % 3
                if h >= 2:
                    v.wait_ge(exp_done, NT * (h - 1))
                for t in range(NT):
                    m = h * NT + t
                    v.wait_ge(score_done, m + 1)
                    d.tensor_tensor_reduce(logit[:, (h % 2 * NT + t) * N:(h % 2 * NT + t + 1) * N],
                                           bank[m % 4][:, 0:N], mask[:, t * N:(t + 1) * N],
                                           1.0, ABSENT * 10, ALU.add, ALU.max,
                                           sm[:, 12 * b + t:12 * b + t + 1]).then_inc(logit_made, 1)
                v.wait_ge(logit_made, NT * (h + 1))
                d.tensor_scalar(sm[:, 12 * b + 3:12 * b + 6], sm[:, 12 * b:12 * b + 3], -SCORE_SCALE, None,
                                ALU.mult).then_inc(negmax, 1)

            def sums(h):
                b = h % 3
                v.wait_ge(exp_done, NT * (h + 1))
                d.reciprocal(sm[:, 12 * b + 9:12 * b + 12], sm[:, 12 * b + 6:12 * b + 9]).then_inc(rsum, 1)

            def take_pt_lo(h):
                b = h % 2
                for m in range(NT):
                    v.wait_ge(pt_hi_made, NT * h + m + 1)
                    s = slice((b * NT + m) * N, (b * NT + m + 1) * N)
                    d.tensor_tensor(pt_lo[:, s], bank[4 + m][:, 0:N], pt_hi[:, s],
                                    ALU.subtract).then_inc(pt_ready, 1)

            def take_o_lo(h):
                v.wait_ge(o_hi_made, h + 1)
                q = slice(DH * (h % 2), DH * (h % 2) + DH)
                s = slice(h // 2 * N, (h // 2 + 1) * N)
                d.scalar_tensor_tensor(o_lo[q, s], bank[7][q, 0:N], bias_col[q, 5 * KT + h // 2:5 * KT + h // 2 + 1],
                                       o_hi[q, s], ALU.add, ALU.subtract).then_inc(o_ready, 1)

            for n in range(4):
                take_v_lo(n)
            logits(0)
            logits(1)
            for n in range(4, 2 * NT):
                take_v_lo(n)
            for i in range(1, H + 4):
                if 2 <= i < H:
                    logits(i)
                if i <= H:
                    sums(i - 1)
                if 3 <= i < H + 3:
                    take_pt_lo(i - 3)
                if i >= 4:
                    take_o_lo(i - 4)

            v.wait_ge(pv_done, H)
            for r in range(R):
                if r >= DIGIT_SLOTS:
                    v.wait_ge(digit_taken, r - DIGIT_SLOTS + 1)
                b = r % DIGIT_SLOTS
                d.tensor_scalar(one_digit[:, b * NT * N:(b + 1) * NT * N], digits[:, :], DIGIT_BITS * r,
                                2 ** DIGIT_BITS - 1, ALU.logical_shift_right, ALU.bitwise_and)\
                 .then_inc(digit_cut, 1)

            v.wait_ge(xres_loaded, 16)
            v.wait_ge(bo_loaded, 16)
            for t in range(NT):
                ins = d.tensor_tensor(x1[:, t * D:(t + 1) * D], x1[:, t * D:(t + 1) * D], row_bias[:, :],
                                      ALU.add)
                after(ins)
            d.tensor_copy(dup_junk[:, 0:1], sm[:, 0:1]).then_inc(xb_made, 1)

            def row_stats(t, half, src):
                after(d.bn_stats(stats[:, 12 * t + 6 * half:12 * t + 6 * half + 6],
                                 src[:, t * D + half * HALF:t * D + (half + 1) * HALF]))

            def norm_stats(t):
                after(d.bn_aggr(mv[:, 2 * t:2 * t + 2], stats[:, 12 * t:12 * t + 12]))
                after(d.tensor_scalar(negmean[:, t:t + 1], mv[:, 2 * t:2 * t + 1], -1.0, None, ALU.mult))
                d.tensor_scalar(vare[:, t:t + 1], mv[:, 2 * t + 1:2 * t + 2], EPS, None,
                                ALU.add).then_inc(var_made, 1)

            def take_x1t_lo(t):
                for half in range(2):
                    v.wait_ge(x1t_hi_made, 2 * t + half + 1)
                    d.tensor_tensor(x1t_tile(x1t_lo, t, half), turned(t, half), x1t_tile(x1t_hi, t, half),
                                    ALU.subtract).then_inc(x1t_ready, 1)

            for t in range(NT):
                if t < NT - 1:
                    v.wait_ge(wo_summed, t + 1)
                else:
                    v.wait_ge(unit_done, U_ROOT)
                for half in range(2):
                    s = slice(t * D + half * HALF, t * D + (half + 1) * HALF)
                    d.tensor_tensor(x1[:, s], bank[2 * t + half][:, :], x1[:, s], ALU.add).then_inc(res_made, 1)
                v.wait_ge(res_made, 2 * (t + 1))
                for half in range(2):
                    row_stats(t, half, x1)
                norm_stats(t)
                if t == 0:
                    v.wait_ge(total_made, 1)
                    after(d.tensor_reduce(digit_total[:, :], bank[7][:, 0:R], AX.X, ALU.add))
                    d.tensor_scalar(counted[:, :], digit_total[:, :], float(E), None,
                                    ALU.is_equal).then_inc(counted_made, 1)
            take_x1t_lo(0)

            def general_counts():
                waited = [0]

                def then(ins):
                    waited[0] += 1
                    ins.then_inc(general, 1)
                    v.wait_ge(general, waited[0])

                for p in range(R // 2):
                    weight = w_rel[:, p * EC:(p + 1) * EC]
                    rel = cols[:, C_REL:C_REL + EC]
                    then(d.tensor_scalar(weight, rel, float(2 * p + 1), float(FIELD), ALU.is_equal, ALU.mult))
                    then(d.scalar_tensor_tensor(weight, rel, float(2 * p), weight, ALU.is_equal, ALU.add))

                def decode(n):
                    half, p = divmod(n, 4)
                    for t in range(NT):
                        m = n * NT + t
                        v.wait_ge(hist_cast, m + 1)
                        both = both_i[:, (m % 2) * N:(m % 2 + 1) * N]
                        then(d.tensor_scalar(low_i[:, :], both, FIELD - 1, None, ALU.bitwise_and))
                        d.tensor_scalar(high_i[:, :], both, FIELD_BITS, None, ALU.logical_shift_right)\
                         .then_inc(hist_decoded, 1)
                        v.wait_ge(hist_decoded, m + 1)
                        for r, part in ((2 * p, low_i), (2 * p + 1, high_i)):
                            q = a_cnt[:, (r * NT + t) * N:(r * NT + t + 1) * N]
                            if half == 0:
                                ins = d.tensor_copy(q, part[:, :])
                            else:
                                ins = d.tensor_tensor(q, q, part[:, :], ALU.add)
                            then(ins)

                used = 2 * EC
                for n in range(8):
                    half, p = divmod(n, 4)
                    c0, c1 = HALVES[half]
                    with v.Fori(0, (c1 - c0) // OH) as i:
                        for j in range(OH):
                            one_hots(i * OH + (c0 + j), i * OH + (used + j), j, w_rel, p * EC)
                    used += c1 - c0
                    if n >= 1:
                        decode(n - 1)
                decode(7)
                d.memset(dup_junk[:, 0:1], 0.0).then_inc(a_made, 1)
                v.wait_ge(a_hi_made, 1)
                d.tensor_tensor(a_lo[:, :], a_cnt[:, :], a_hi[:, :], ALU.subtract).then_inc(a_ready, 1)

            v.wait_ge(counted_made, 1)
            stands = v.value_load(counted[0:1, 0:1], min_val=0, max_val=1)
            with v.If(stands == 0):
                general_counts()
            for t in range(1, NT):
                take_x1t_lo(t)
            v.wait_ge(x1h_hi_made, 1)
            d.tensor_tensor(x1h_lo[:, :], x1[:, :], x1h_hi[:, :], ALU.subtract).then_inc(x1h_ready, 1)
            v.wait_ge(cnt_taken, R)
            after(d.tensor_scalar(rcount[:, :], rcount[:, :], 1.0, None, ALU.max))
            d.reciprocal(rcount[:, :], rcount[:, :]).then_inc(rc_made, 1)
            v.wait_ge(rc_made, 1)

            with v.Fori(0, R) as r:
                for k in range(KT):
                    n = r * KT + (k + 1)
                    b = k % 2
                    v.wait_ge(agg_done, n)
                    d.tensor_tensor(bank[6 + b][:, 0:N], bank[6 + b][:, 0:N], rcount[:, bass.ds(r * N, N)],
                                    ALU.mult).then_inc(mean_scaled, 1)
                    v.wait_ge(mean_hi_made, n)
                    d.tensor_tensor(mean_lo[:, b * N:(b + 1) * N], bank[6 + b][:, 0:N],
                                    mean_hi[:, b * N:(b + 1) * N], ALU.subtract).then_inc(mean_ready, 1)
            v.wait_ge(rb_loaded, 16)
            for n in range(2 * NT):
                if n // 2 < NT - 1:
                    v.wait_ge(u_summed, n // 2 + 1)
                else:
                    v.wait_ge(unit_done, U_GX)
                s = slice(n * HALF, (n + 1) * HALF)
                d.tensor_tensor(u_nat[:, s], bank[n][:, :], row_bias[:, (n % 2) * HALF:(n % 2 + 1) * HALF],
                                ALU.add).then_inc(u_made, 1)
            for k in range(KT):
                v.wait_ge(ut_hi_made, k + 1)
                s = slice(k * N, (k + 1) * N)
                d.tensor_tensor(ut_lo[:, s], bank[6 + k % 2][:, 0:N], ut_hi[:, s],
                                ALU.subtract).then_inc(ut_ready, 1)
            v.wait_ge(unit_done, U_GX)
            after(d.tensor_tensor(x1[:, :], x1h_hi[:, :], x1h_lo[:, :], ALU.add))
            v.wait_ge(bg_loaded, 16)
            for t in range(NT):
                s = slice(t * D, (t + 1) * D)
                v.wait_ge(tanh_made, t + 1)
                after(d.tensor_tensor(gated[:, s], gated[:, s], x1[:, s], ALU.subtract))
                after(d.tensor_tensor(fixed[:, s], gated[:, s], row_bias[:, :], ALU.mult))
                after(d.scalar_tensor_tensor(fixed[:, s], x1[:, s], 2.0, fixed[:, s], ALU.mult, ALU.add))
            v.wait_ge(hi_split, UNITS)
            v.wait_ge(lo_split, UNITS - 1)
            s = slice((RING - 1) * UNIT, RING * UNIT)
            d.tensor_tensor(w_lo[:, s], raw[:, s], w_hi[:, s], ALU.subtract).then_inc(lo_split, 1)
            for t in range(NT):
                for half in range(2):
                    s = slice(t * D + half * HALF, t * D + (half + 1) * HALF)
                    v.wait_ge(z_summed, 2 * t + half + 1)
                    after(d.tensor_tensor(result[:, s], bank[2 * t + half][:, :], gated[:, s], ALU.mult))
                    after(d.tensor_tensor(result[:, s], result[:, s], fixed[:, s], ALU.add))
                    row_stats(t, half, result)
                norm_stats(t)

        @block.tensor
        def _(pe):
            mm = nc.tensor.matmul

            def three(dst, l_hi, l_lo, r_hi, r_lo, start, stop):
                mm(dst, l_hi, r_hi, start=start, stop=False)
                mm(dst, l_hi, r_lo, start=False, stop=False)
                return mm(dst, l_lo, r_hi, start=False, stop=stop)

            def f_unit(u, j, src_hi, src_lo, at, piecewise=False, halfway=None):
                pe.wait_ge(lo_split, u + 1)
                for k in range(KT):
                    if halfway and k == KT // 2:
                        halfway()
                    if piecewise and k % (KT // XC) == 0:
                        pe.wait_ge(x_ready, k // (KT // XC) + 1)
                    w = slice((j % RING) * UNIT + k * P, (j % RING) * UNIT + (k + 1) * P)
                    m = bass.ds(at + k * N, N)
                    last = three(bank[j % RING][:, 0:N], w_hi[:, w], w_lo[:, w], src_hi[:, m], src_lo[:, m],
                                 k == 0, k == KT - 1)
                last.then_inc(unit_done, 1)

            pe.wait_ge(warm_zeros, 1)
            with pe.Fori(0, WARM_UP // 4):
                for _ in range(4):
                    mm(bank[7][:, 0:N], src_oh[:, 0:P], src_oh[:, 0:N], start=True, stop=True)
            pe.wait_ge(f_lo, 1)
            f_unit(0, 0, xt_hi, xt_lo, 0, piecewise=True)
            for j in range(1, KT):
                pe.wait_ge(f_lo, j + 1)
                f_unit(j, j, xt_hi, xt_lo, 0)
                if j == 2:
                    pe.wait_ge(rows_cast, 4)
                    pe.wait_ge(const_made, 7)
                    for n in range(4):
                        nc.tensor.transpose(bank[7][:, n * EC:(n + 1) * EC], erow_f[:, n * P:(n + 1) * P],
                                            ident[0:EC, 0:EC]).then_inc(cols_turned, 1)

            def chunk(n, slot, start, stop, first=4):
                pe.wait_ge(oh_ready, (n + 1) * 2)
                m = slice(slot * N, (slot + 1) * N)
                for t in range(NT):
                    last = mm(bank[first + t][:, 0:N], src_oh[:, slot * N + t * P:slot * N + (t + 1) * P],
                              dst_oh[:, m], start=start, stop=stop)
                last.then_inc(oh_used, 1)

            for j in range(RING):
                pe.wait_ge(f_lo, KT + j + 1)
                f_unit(KT + j, j, xt_hi, xt_lo, 0)
                for c in range(OH):
                    chunk(j * OH + c, c, j == 0 and c == 0, False)
            with pe.Fori(1, 2 * KT // RING) as i:
                for j in range(RING):
                    pe.wait_ge(f_lo, i * RING + (KT + j + 1))
                    f_unit(i * RING + (KT + j), j, xt_hi, xt_lo, 0)
                    for c in range(OH):
                        chunk(i * (RING * OH) + (j * OH + c), c, False, False)
            pe.wait_ge(f_lo, U_F2 + RING - KT)
            for j in range(KT):
                pe.wait_ge(f_lo, U_F2 + j + 1)
                groups = [range(g * OH, (g + 1) * OH) for g in range(sum(MASK_GROUPS[:j]), sum(MASK_GROUPS[:j + 1]))]

                def mask_chunks():
                    for n in groups.pop(0):
                        if n == 0:
                            pe.wait_ge(digits_saved, NT)
                        chunk(EC + n, n % OH, n == 0, False)

                f_unit(U_F2 + j, j, t1_hi, t1_lo, 0, halfway=mask_chunks if len(groups) > 1 else None)
                if j == 0:
                    for n in range(2 * OH * KT, EC):
                        chunk(n, n % OH, False, n == EC - 1)
                if groups:
                    mask_chunks()
            with pe.Fori(0, KT // RING) as i:
                for j in range(RING):
                    pe.wait_ge(f_lo, i * RING + (U_F2 + KT + j + 1))
                    f_unit(i * RING + (U_F2 + KT + j), j, t1_hi, t1_lo, ACTS)
                    for c in range(OH):
                        n = i * (RING * OH) + ((MASK_BEFORE_K2 + j) * OH + c)
                        chunk(n + EC, c, False, False)
            def scores(h):
                q = slice(DH * (h % 2), DH * (h % 2) + DH)
                for t in range(NT):
                    m = h * NT + t
                    if m >= 4:
                        pe.wait_ge(logit_made, m - 3)
                    else:
                        pe.wait_ge(v_ready, m + 1)
                    n0 = h // 2 * N
                    sq = slice(n0 + t * P, n0 + (t + 1) * P)
                    sk = slice(ACTS + n0, ACTS + n0 + N)
                    three(bank[m % 4][:, 0:N], t2_hi[q, sq], t2_lo[q, sq], t2_hi[q, sk], t2_lo[q, sk],
                          True, True).then_inc(score_done, 1)

            def turn_p(h):
                b = h % 3
                for m in range(NT):
                    if h == 0:
                        pe.wait_ge(v_ready, 2 * NT)
                    if h >= 1:
                        pe.wait_ge(pt_ready, NT * (h - 1) + m + 1)
                    for t in range(NT):
                        pe.wait_ge(prob_ready, NT * h + t + 1)
                        s0 = t * N + m * P
                        last = nc.tensor.transpose(bank[4 + m][:, t * P:(t + 1) * P],
                                                   prob[b][:, s0:s0 + P], ident[:, :])
                    last.then_inc(p_turned, 1)

            def weigh_v(h):
                b = h % 2
                if h >= 1:
                    pe.wait_ge(o_ready, h)
                for m in range(NT):
                    pe.wait_ge(pt_ready, NT * h + m + 1)
                    sv = slice(m * D + h // 2 * P, m * D + (h // 2 + 1) * P)
                    s = slice((b * NT + m) * N, (b * NT + m + 1) * N)
                    last = three(bank[7][:, 0:N], v2_hi[:, sv], v2_lo[:, sv], pt_hi[:, s], pt_lo[:, s],
                                 m == 0, m == NT - 1)
                last.then_inc(pv_done, 1)

            def n_tile(w0, l_hi, l_lo, at, t, start, stop):
                s = slice(at + t * P, at + (t + 1) * P)
                for half in range(2):
                    w = slice(w0 + half * HALF, w0 + (half + 1) * HALF)
                    last = three(bank[2 * t + half][:, :], l_hi[:, s], l_lo[:, s], w_hi[:, w],
                                 w_lo[:, w], start, stop)
                return last

            def n_unit(u, l_hi, l_lo, k, start, stop, wait_tile=None, at=0):
                pe.wait_ge(lo_split, u + 1)
                for t in range(NT):
                    if wait_tile:
                        wait_tile(t)
                    last = n_tile(u % RING * UNIT, l_hi, l_lo, at + k * N, t, start, stop)
                last.then_inc(unit_done, 1)

            for t in range(NT):
                if t < NT - 1:
                    pe.wait_ge(f_lo, U_V2 + RING - 2 + 2 * t)
                else:
                    pe.wait_ge(mask_read, NT)
                for k in range(2):
                    if t == 0:
                        pe.wait_ge(lo_split, U_V2 + k + 1)
                    last = n_tile(k * UNIT, t1_hi, t1_lo, 2 * ACTS + k * N, t, k == 0, False)
                    if t == NT - 1:
                        last.then_inc(unit_done, 1)
                if t == 0:
                    for n in range(EC - OH, EC):
                        chunk(EC + n, n % OH, False, n == EC - 1)
            for k in range(2, KT - 2):
                n_unit(U_V2 + k, t1_hi, t1_lo, k, False, False, at=2 * ACTS)
            for t in range(NT):
                for k in range(KT - 2, KT):
                    if t == NT - 1 and k == KT - 1:
                        scores(0)
                        scores(1)
                    if t == 0:
                        pe.wait_ge(lo_split, U_V2 + k + 1)
                    last = n_tile(k % RING * UNIT, t1_hi, t1_lo, 2 * ACTS + k * N, t, False, k == KT - 1)
                    if t == NT - 1 and k < KT - 1:
                        last.then_inc(unit_done, 1)
                last.then_inc(v_summed if t < NT - 1 else unit_done, 1)

            for i in range(2, H + 4):
                if i < H:
                    scores(i)
                else:
                    k = i - H
                    pe.wait_ge(logit_made, NT * H)
                    pe.wait_ge(o_ready, 2 * k + 2)
                    pe.wait_ge(lo_split, U_WO + k + 1)
                    n_tile(k * UNIT, o_hi, o_lo, k * N, 0, k == 0, False)
                if 3 <= i < H + 3:
                    turn_p(i - 3)
                if i >= H:
                    n_tile(k * UNIT, o_hi, o_lo, k * N, 1, k == 0, False)
                if i >= 4:
                    weigh_v(i - 4)
            pe.wait_ge(pt_ready, NT * H)
            for k in range(4):
                n_tile(k * UNIT, o_hi, o_lo, k * N, 2, k == 0, False).then_inc(unit_done, 1)
            for k in range(4, KT - 2):
                pe.wait_ge(o_ready, 2 * k + 2)
                n_unit(U_WO + k, o_hi, o_lo, k, False, False)
            pe.wait_ge(o_ready, H)
            for t in range(NT):
                for k in range(KT - 2, KT):
                    if t == 0:
                        pe.wait_ge(lo_split, U_WO + k + 1)
                    last = n_tile(k % RING * UNIT, o_hi, o_lo, k * N, t, False, k == KT - 1)
                    if t == NT - 1 and k < KT - 1:
                        last.then_inc(unit_done, 1)
                last.then_inc(wo_summed if t < NT - 1 else unit_done, 1)
                if t == 0:
                    pe.wait_ge(digit_taken, R)
                    mm(bank[7][:, 0:R], ones[:, :], digit_sum[:, :], start=True, stop=True).then_inc(total_made, 1)

            def turn_x1(t):
                pe.wait_ge(x1_made, t + 1)
                for half in range(2):
                    for q in range(KT // 2):
                        k = half * (KT // 2) + q
                        last = nc.tensor.transpose(turned(t, half)[:, q, :], x1[:, t * D + k * P:t * D + (k + 1) * P],
                                                   ident[:, :])
                    last.then_inc(x1_turned, 1)

            pe.wait_ge(counted_made, 1)
            turn_x1(0)
            stands = pe.value_load(counted[0:1, 0:1], min_val=0, max_val=1)

            def count(r, with_lo):
                if r >= CNT_BANKS:
                    pe.wait_ge(cnt_taken, r - CNT_BANKS + 1)
                dst = bank[2 + r % CNT_BANKS][:, 0:N]
                for t in range(NT):
                    m = slice((r * NT + t) * N, (r * NT + t + 1) * N)
                    last = mm(dst, ones_r[:, :], a_hi[:, m], start=t == 0, stop=t == NT - 1 and not with_lo)
                if with_lo:
                    for t in range(NT):
                        m = slice((r * NT + t) * N, (r * NT + t + 1) * N)
                        last = mm(dst, ones_r[:, :], a_lo[:, m], start=False, stop=t == NT - 1)
                last.then_inc(cnt_summed, 1)

            pe.wait_ge(res_made, 2 * NT)
            pe.wait_ge(ones_made, 1)
            with pe.If(stands == 0):
                used = 2 * EC
                for n in range(8):
                    c0, c1 = HALVES[n // 4]
                    first = (n % 2) * NT
                    if n >= 2:
                        pe.wait_ge(hist_cast, NT * (n - 1))
                    for j in range(OH):
                        chunk(used + j, j, j == 0, False, first)
                    with pe.Fori(1, (c1 - c0) // OH - 1) as i:
                        for j in range(OH):
                            chunk(i * OH + (used + j), j, False, False, first)
                    for j in range(OH):
                        chunk(used + c1 - c0 - OH + j, j, False, j == OH - 1, first)
                    used += c1 - c0
                pe.wait_ge(a_ready, 1)
                for r in range(R):
                    count(r, True)
            with pe.Else():
                for r in range(R):
                    count(r, False)
            for t in range(NT):
                if t == 0:
                    pe.wait_ge(x1t_ready, 2)
                    turn_x1(1)
                elif t == 1:
                    pe.wait_ge(cnt_taken, R)
                    turn_x1(2)
                    pe.wait_ge(x1t_ready, 4)
                else:
                    pe.wait_ge(x1t_ready, 6)
                for k in range(2):
                    if t == 0:
                        pe.wait_ge(lo_split, U_ROOT + k + 1)
                    last = n_tile(k * UNIT, x1t_hi, x1t_lo, k * N, t, k == 0, False)
                    if t == NT - 1:
                        last.then_inc(unit_done, 1)
            for k in range(2, KT - 1):
                n_unit(U_ROOT + k, x1t_hi, x1t_lo, k, False, False)

            def sum_edges(k, at, with_lo):
                dst = bank[6 + k % 2][:, 0:N]
                for s_ in range(NT):
                    s = slice(s_ * D + k * P, s_ * D + (k + 1) * P)
                    m = slice(at + s_ * N, at + (s_ + 1) * N) if isinstance(at, int) else bass.ds(at + s_ * N, N)
                    mm(dst, x1h_hi[:, s], a_hi[:, m], start=s_ == 0, stop=False)
                    if with_lo:
                        mm(dst, x1h_hi[:, s], a_lo[:, m], start=False, stop=False)
                    last = mm(dst, x1h_lo[:, s], a_hi[:, m], start=False, stop=s_ == NT - 1)
                last.then_inc(agg_done, 1)

            def relations(with_lo):
                def aggregate(n, k, at):
                    pe.wait_ge(mean_ready, n)
                    sum_edges(k, at, with_lo)

                def weigh_mean(n, k):
                    pe.wait_ge(mean_ready, n + 2)
                    pe.wait_ge(lo_split, n + (U_REL + 1))
                    for t in range(NT):
                        last = n_tile(k % RING * UNIT, mean_hi, mean_lo, k % 2 * N, t, False, False)
                    last.then_inc(unit_done, 1)

                sum_edges(0, 0, with_lo)
                n_unit(U_REL - 1, x1t_hi, x1t_lo, KT - 1, False, False)
                with pe.Fori(0, R - 1) as r:
                    for k in range(KT):
                        n = r * KT + k
                        aggregate(n + 1, (k + 1) % KT, (r + (1 if k == KT - 1 else 0)) * (NT * N))
                        weigh_mean(n, k)
                n0 = (R - 1) * KT
                for k in range(KT - 2):
                    aggregate(n0 + k + 1, k + 1, (R - 1) * NT * N)
                    if k == KT - 3:
                        aggregate(n0 + KT - 1, KT - 1, (R - 1) * NT * N)
                    weigh_mean(n0 + k, k)
                for t in range(NT):
                    for k in range(KT - 2, KT):
                        if t == 0:
                            pe.wait_ge(mean_ready, n0 + k + 2)
                            pe.wait_ge(lo_split, n0 + k + U_REL + 1)
                        last = n_tile(k % RING * UNIT, mean_hi, mean_lo, k % 2 * N, t, False, k == KT - 1)
                        if t == NT - 1 and k < KT - 1:
                            last.then_inc(unit_done, 1)
                    last.then_inc(u_summed if t < NT - 1 else unit_done, 1)

            pe.wait_ge(x1h_ready, 1)
            with pe.If(stands == 0):
                relations(True)
            with pe.Else():
                relations(False)

            for k in range(KT):
                n_unit(U_GX + k, x1t_hi, x1t_lo, k, k == 0, False,
                       (lambda t: pe.wait_ge(u_made, 2 * t + 2)) if k == 0 else None)
                for kk in range(2 * k, min(2 * k + 2, KT)):
                    if kk >= 2:
                        pe.wait_ge(ut_ready, kk - 1)
                    for t in range(NT):
                        last = nc.tensor.transpose(
                            bank[6 + kk % 2][:, t * P:(t + 1) * P],
                            u_nat[:, t * D + kk * P:t * D + (kk + 1) * P], ident[:, :])
                    last.then_inc(u_turned, 1)
            pe.wait_ge(ut_ready, KT)
            for k in range(KT - RING):
                n_unit(U_GU + k, ut_hi, ut_lo, k, False, False)
            for n in range(2 * NT):
                t, half = divmod(n, 2)
                for k in range(KT - RING, KT):
                    if n == 0:
                        pe.wait_ge(lo_split, U_GU + k + 1)
                    l = slice(k * N + t * P, k * N + (t + 1) * P)
                    w = slice(k % RING * UNIT + half * HALF, k % RING * UNIT + (half + 1) * HALF)
                    last = three(bank[n][:, :], ut_hi[:, l], ut_lo[:, l], w_hi[:, w], w_lo[:, w],
                                 False, k == KT - 1)
                last.then_inc(z_summed, 1)


def kernel(**inputs):
    import numpy as np
    import concourse.bacc as bacc
    from concourse.bass_utils import run_bass_kernel_spmd as run

    i = {k: np.asarray(v) for k, v in inputs.items()}
    p, n, d = 128, 384, 1024
    kt, nt = d // p, n // p
    e = i["src"].shape[0]

    def f_order(w):
        return w.reshape(kt, p, kt, p).transpose(0, 3, 2, 1).reshape(kt, p, d)

    def n_order(w):
        return w.reshape(kt, p, d)

    g = {k[7:]: v for k, v in i.items() if k.startswith("L")}
    weights = np.concatenate(
        [f_order(g[k]) for k in ("wq", "wk", "wv", "wiq", "wik")]
        + [n_order(g["wiv"].T), n_order(g["wo"].T), n_order(g["root"])]
        + [n_order(w) for w in g["weight"]]
        + [n_order(g["w_gate"][d:]), n_order(g["w_gate"][:d])])
    arrays = {
        "x_nat": i["x"].reshape(nt, p, d).transpose(1, 0, 2).reshape(p, nt * d),
        "x_t": i["x"].T.reshape(kt, p, n).transpose(1, 0, 2).reshape(p, kt * n),
        "edges": np.concatenate([i[k].reshape(e // p, p) for k in ("src", "dst", "edge_type_5", "edge_type_8")], 1),
        "keys_src": i["src"], "keys_dst": i["dst"],
        "type_w": g["edge_type_weights"],
        "bias_f": np.concatenate([g[k].reshape(kt, p) for k in ("bq", "bk", "bv", "biq", "bik", "biv")]).T,
        "bo": g["bo"], "bias": g["bias"], "b_gate": g["b_gate"],
        "weights": weights,
    }
    arrays = {k: np.ascontiguousarray(v) for k, v in arrays.items()}
    nc = bacc.Bacc("TRN2", target_bir_lowering=False, num_devices=1)
    args = [nc.dram_tensor(k, v.shape, mybir.dt.from_np(v.dtype), kind="ExternalInput").ap()
            for k, v in arrays.items()]
    out = nc.dram_tensor("out_dram", (nt, p, d), mybir.dt.float32, kind="ExternalOutput").ap()
    build(nc, *args, out)
    r = run(nc, [arrays], core_ids=[0])
    return np.asarray(r.results[0]["out_dram"]).reshape(n, d)
```
